# Optimizing a Trainium2 kernel written in Bass

```python
import numpy as np
import jax
import jax.numpy as jnp

def _softmax(x, axis=-1):
    return jax.nn.softmax(x, axis=axis)

def _gelu(x):
    return jax.nn.gelu(x, approximate=True)

def _silu(x):
    return jax.nn.silu(x)

def _sigmoid(x):
    return jax.nn.sigmoid(x)

def _layernorm(x, axis=-1, eps=1e-05):
    m = jnp.mean(x, axis=axis, keepdims=True)
    v = jnp.var(x, axis=axis, keepdims=True)
    return (x - m) / jnp.sqrt(v + eps)

def _scatter_add(tgt, idx, src, axis=0):
    return tgt.at[idx].add(src)

def _segment_sum(src, seg, n):
    return jax.ops.segment_sum(src, seg, n)
kernel_name = 'mk_prb_d1_jaxref_r8_7519e2'

def setup_inputs(seed: int=0):
    np.random.seed(seed)
    _w = jnp.asarray

    def _L0_attn_setup():
        import jax, jax.numpy as jnp
        import numpy as np
        import math
        D_MODEL = 128
        N_HEADS = 16
        D_K = D_MODEL // N_HEADS
        BATCH = 4
        SEQ = 256
        TRAINING_PROGRESS = 0.25
        CONVERGENCE_PHASE = 0.5
        TENSION = abs(1.0 - 1.0)

        def _pos_encoding(seq_len, d, yellow):
            phase_mod = 0.1 * math.sin(2.0 * math.pi * TRAINING_PROGRESS)
            i_even = jnp.arange(0, d, 2, dtype=jnp.float32)
            denom = jnp.power(10000.0, 2.0 * i_even / d) * (1.0 + yellow * phase_mod)
            pos = jnp.arange(seq_len, dtype=jnp.float32)
            ang = pos[:, None] / denom[None, :]
            pe = jnp.zeros((seq_len, d), jnp.float32)
            pe = pe.at[:, 0::2].set(jnp.sin(ang))
            pe = pe.at[:, 1::2].set(jnp.cos(ang))
            return pe
        key = jax.random.key(seed)
        ks = jax.random.split(key, 8)
        x = jax.random.normal(ks[0], (BATCH, SEQ, D_MODEL), dtype=jnp.float32)
        rby = jax.random.uniform(ks[1], (3,), dtype=jnp.float32)
        s = 0.02
        Wq = jax.random.normal(ks[2], (D_MODEL, D_MODEL), dtype=jnp.float32) * s
        Wk = jax.random.normal(ks[3], (D_MODEL, D_MODEL), dtype=jnp.float32) * s
        Wv = jax.random.normal(ks[4], (D_MODEL, D_MODEL), dtype=jnp.float32) * s
        Wo = jax.random.normal(ks[5], (D_MODEL, D_MODEL), dtype=jnp.float32) * s
        bq = jnp.zeros((D_MODEL,), jnp.float32)
        bk = jnp.zeros((D_MODEL,), jnp.float32)
        bv = jnp.zeros((D_MODEL,), jnp.float32)
        bo = jnp.zeros((D_MODEL,), jnp.float32)
        ln_gamma = jnp.ones((D_MODEL,), jnp.float32)
        ln_beta = jnp.zeros((D_MODEL,), jnp.float32)
        return {'x': x, 'rby': rby, 'Wq': Wq, 'bq': bq, 'Wk': Wk, 'bk': bk, 'Wv': Wv, 'bv': bv, 'Wo': Wo, 'bo': bo, 'ln_gamma': ln_gamma, 'ln_beta': ln_beta}
    _L0_attn_in = _L0_attn_setup()

    def _L0_ffn_setup():
        import jax, jax.numpy as jnp
        import numpy as np
        HIDDEN = 128
        FFN = 4 * HIDDEN
        NUM_EXPERTS = 8
        TOP_K = 2
        B, S = (4, 256)
        key = jax.random.key(seed)
        ks = jax.random.split(key, 7)
        scale = 0.02
        return {'x': jax.random.normal(ks[0], (B, S, HIDDEN), dtype=jnp.float32), 'gate_w': jax.random.normal(ks[1], (HIDDEN, NUM_EXPERTS), dtype=jnp.float32) * scale, 'gate_b': jnp.zeros((NUM_EXPERTS,), dtype=jnp.float32), 'w1': jax.random.normal(ks[2], (NUM_EXPERTS, HIDDEN, FFN), dtype=jnp.float32) * scale, 'b1': jnp.zeros((NUM_EXPERTS, FFN), dtype=jnp.float32), 'w2': jax.random.normal(ks[3], (NUM_EXPERTS, FFN, HIDDEN), dtype=jnp.float32) * scale, 'b2': jnp.zeros((NUM_EXPERTS, HIDDEN), dtype=jnp.float32)}
    _L0_ffn_in = _L0_ffn_setup()
    _d = {'L0_attn_x': _L0_attn_in['x'], 'L0_attn_rby': _L0_attn_in['rby'], 'L0_attn_Wq': _L0_attn_in['Wq'], 'L0_attn_bq': _L0_attn_in['bq'], 'L0_attn_Wk': _L0_attn_in['Wk'], 'L0_attn_bk': _L0_attn_in['bk'], 'L0_attn_Wv': _L0_attn_in['Wv'], 'L0_attn_bv': _L0_attn_in['bv'], 'L0_attn_Wo': _L0_attn_in['Wo'], 'L0_attn_bo': _L0_attn_in['bo'], 'L0_attn_ln_gamma': _L0_attn_in['ln_gamma'], 'L0_attn_ln_beta': _L0_attn_in['ln_beta'], 'L0_ffn_gate_w': _L0_ffn_in['gate_w'], 'L0_ffn_gate_b': _L0_ffn_in['gate_b'], 'L0_ffn_w1': _L0_ffn_in['w1'], 'L0_ffn_b1': _L0_ffn_in['b1'], 'L0_ffn_w2': _L0_ffn_in['w2'], 'L0_ffn_b2': _L0_ffn_in['b2']}
    _x0 = _d['L0_attn_x']
    _d['L0_attn_x'] = jax.random.normal(jax.random.fold_in(jax.random.key(seed), 1), (4, 1024, 128), dtype=_x0.dtype)
    del _x0
    return _d

def reference(L0_attn_x, L0_attn_rby, L0_attn_Wq, L0_attn_bq, L0_attn_Wk, L0_attn_bk, L0_attn_Wv, L0_attn_bv, L0_attn_Wo, L0_attn_bo, L0_attn_ln_gamma, L0_attn_ln_beta, L0_ffn_gate_w, L0_ffn_gate_b, L0_ffn_w1, L0_ffn_b1, L0_ffn_w2, L0_ffn_b2):

    def _L0_attn_ref(x, rby, Wq, bq, Wk, bk, Wv, bv, Wo, bo, ln_gamma, ln_beta):
        import jax, jax.numpy as jnp
        import numpy as np
        import math
        D_MODEL = 128
        N_HEADS = 16
        D_K = D_MODEL // N_HEADS
        BATCH = 4
        SEQ = 256
        TRAINING_PROGRESS = 0.25
        CONVERGENCE_PHASE = 0.5
        TENSION = abs(1.0 - 1.0)

        def _pos_encoding(seq_len, d, yellow):
            phase_mod = 0.1 * math.sin(2.0 * math.pi * TRAINING_PROGRESS)
            i_even = jnp.arange(0, d, 2, dtype=jnp.float32)
            denom = jnp.power(10000.0, 2.0 * i_even / d) * (1.0 + yellow * phase_mod)
            pos = jnp.arange(seq_len, dtype=jnp.float32)
            ang = pos[:, None] / denom[None, :]
            pe = jnp.zeros((seq_len, d), jnp.float32)
            pe = pe.at[:, 0::2].set(jnp.sin(ang))
            pe = pe.at[:, 1::2].set(jnp.cos(ang))
            return pe
        B, S, d = x.shape
        red, blue, yellow = (rby[0], rby[1], rby[2])
        x = x + _pos_encoding(S, d, yellow)[None, :, :]

        def proj(W, b):
            return (x @ W.T + b).reshape(B, S, N_HEADS, D_K).transpose(0, 2, 1, 3)
        Q, K, V = (proj(Wq, bq), proj(Wk, bk), proj(Wv, bv))
        scale = jnp.sqrt(D_K * (1.0 + TENSION * red))
        logits = jnp.einsum('bhqd,bhkd->bhqk', Q, K) / scale
        scale_matrix = 1.0 + red * 0.1 + blue * 0.05 + yellow * 0.15
        logits = logits * scale_matrix
        attn = jax.nn.softmax(logits, axis=-1)
        eps_adaptive = 0.1 * math.sin(2.0 * math.pi * CONVERGENCE_PHASE)
        out = jnp.einsum('bhqk,bhkd->bhqd', attn, V) * (1.0 + yellow * eps_adaptive)
        out = out.transpose(0, 2, 1, 3).reshape(B, S, d)
        out = out @ Wo.T + bo
        x = x + out
        mean = jnp.mean(x, axis=-1, keepdims=True)
        var = jnp.var(x, axis=-1, keepdims=True)
        eps_rby = 1e-05 * (1.0 + blue * 0.1)
        gamma_rby = ln_gamma * (1.0 + red * 0.1 + yellow * 0.05)
        normalized = (x - mean) / jnp.sqrt(var + eps_rby)
        return normalized * gamma_rby + ln_beta

    def _L0_ffn_ref(x, gate_w, gate_b, w1, b1, w2, b2):
        import jax, jax.numpy as jnp
        import numpy as np
        HIDDEN = 128
        FFN = 4 * HIDDEN
        NUM_EXPERTS = 8
        TOP_K = 2
        B, S = (4, 256)
        b, s, h = x.shape
        xt = x.reshape(b * s, h)
        probs = jax.nn.softmax(xt @ gate_w + gate_b, axis=-1)
        _, idx = jax.lax.top_k(probs, TOP_K)
        one_hot = jax.nn.one_hot(idx, NUM_EXPERTS, dtype=xt.dtype)
        mask = (one_hot.sum(axis=1) > 0).astype(xt.dtype)
        h1 = jax.nn.relu(jnp.einsum('th,ehf->etf', xt, w1) + b1[:, None, :])
        out_e = jnp.einsum('etf,efh->eth', h1, w2) + b2[:, None, :]
        out = jnp.einsum('eth,te->th', out_e, mask)
        return out.reshape(b, s, h)
    x = L0_attn_x
    xn = _layernorm(x, axis=-1)
    x = x + _L0_attn_ref(xn, L0_attn_rby, L0_attn_Wq, L0_attn_bq, L0_attn_Wk, L0_attn_bk, L0_attn_Wv, L0_attn_bv, L0_attn_Wo, L0_attn_bo, L0_attn_ln_gamma, L0_attn_ln_beta) + _L0_ffn_ref(xn, L0_ffn_gate_w, L0_ffn_gate_b, L0_ffn_w1, L0_ffn_b1, L0_ffn_w2, L0_ffn_b2)
    return x

_drawn_inputs = setup_inputs


def setup_inputs(seed=0):
    import zlib

    import numpy as np

    out = dict(_drawn_inputs(seed))
    spreads = {'L0_attn_bq': (0.0, 0.8),
     'L0_attn_bk': (0.0, 0.8),
     'L0_attn_bv': (0.0, 0.787),
     'L0_attn_bo': (0.0, 0.1),
     'L0_attn_ln_gamma': (1.0, 0.2),
     'L0_attn_ln_beta': (0.0, 0.1),
     'L0_ffn_gate_b': (0.0, 0.1),
     'L0_ffn_b1': (0.0, 0.371),
     'L0_ffn_b2': (0.0, 0.1)}
    factors = {'L0_attn_Wq': 8.0, 'L0_attn_Wk': 8.0, 'L0_attn_Wv': 4.215, 'L0_attn_Wo': 3.356}
    for name, (base, spread) in spreads.items():
        noise = np.random.default_rng([zlib.crc32(name.encode()), seed]).standard_normal(out[name].shape)
        drawn = base * np.exp(spread * noise) if base else spread * noise
        out[name] = jnp.asarray(drawn.astype(out[name].dtype))
    for name, factor in factors.items():
        out[name] = (out[name] * factor).astype(out[name].dtype)
    return out
```

```python
from contextlib import ExitStack

import concourse.bass as bass
from concourse import mybir

F32 = mybir.dt.float32
BF16 = mybir.dt.bfloat16
ALU = mybir.AluOpType
ACT = mybir.ActivationFunctionType
AX_X = mybir.AxisListType.X

P = 128
B, S, D = 4, 1024, 128
H, DK = 16, 8
NT = S // P
E, F = 8, 512
FT = F // P
CH = 512
NC = S // CH
U = 4
NG = H // U
NU = B * NG
NW = NU * NC
PARTS = 3
PROD = PARTS * PARTS * DK
KR = 96
KR2 = KR + PARTS
RING = 4
HALF = 2 * S
ITEMS = 16
LEAD = 3
PI = 3.14159265358979
PI_DOWN = 3.1415925
FRONT_STEPS = 36
CHUNK_STEPS = E - 2
PARTS_STORES = 2 * PARTS * NG * 16
TAIL_STEPS = 16
TENSION = abs(1.0 - 1.0)
PHASE = 0.1
EPS_ADAPTIVE = 0.1 * 1.2246467991473532e-16
ROUND = 1.5 * 2.0 ** 23
TWO_PI_HI = 6.28125
TWO_PI_LO = 6.283185307179586 - 6.28125


class Chain:

    def __init__(self, eng, sem):
        self.eng, self.sem, self.n, self.base, self.outer = eng, sem, 0, 0, []

    def done(self, ins):
        ins.then_inc(self.sem, 1)
        self.n += 1

    def settle(self):
        self.eng.wait_ge(self.sem, self.base + self.n)

    def link(self, ins):
        self.done(ins)
        self.settle()

    def turn(self, i, per_turn):
        self.outer.append((self.base, self.n, per_turn))
        self.base = self.base + i * per_turn

    def end_turns(self, turns):
        self.base, start, per_turn = self.outer.pop()
        assert self.n - start == per_turn, (self.n - start, per_turn)
        self.n = start + turns * per_turn


def row(vec, n=P):
    return vec.partition_broadcast(n)


def build(nc, x, rby, wqT, bq, wkT, bk, wvT, bv, woT, bo, gamma, beta, gate_w, gate_b, w1, b1T, w2, b2T,
          ident_in, freq, pos, rank_in, out):
    with ExitStack() as whole:
        def sb(ctx, name, shape, dt=F32):
            return ctx.enter_context(nc.sbuf_tensor(name, shape, dt))

        def sem(name):
            return whole.enter_context(nc.semaphore(name))

        qk_parts = nc.dram_tensor("qk_parts", (2, NU, PARTS, DK, U, S), BF16, kind="Internal").ap()
        mask_rows = nc.dram_tensor("mask_rows", (B, E, S), BF16, kind="Internal").ap()
        attn_sums = nc.dram_tensor("attn_sums", (2, B, P, S), F32, kind="Internal").ap()

        bank = whole.enter_context(nc.psum_tensor("bank", [P, 8, CH], F32))

        X = sb(whole, "X", [P, B * NT, D])
        XP = sb(whole, "XP", [P, B * NT, D])
        V = sb(whole, "V", [P, B * NT, D])
        ident = sb(whole, "ident", [P, P])
        wo = sb(whole, "wo", [P, D])
        bo_row = sb(whole, "bo_row", [P, D])
        gam_row = sb(whole, "gam_row", [P, D])
        beta_row = sb(whole, "beta_row", [P, D])
        coef = sb(whole, "coef", [P, 16])
        RED, BLUE, YELLOW, QSCALE, LN_EPS, OUT_FACTOR, DEN2, ROOT, TMP, GAM = (coef[:, i:i + 1] for i in range(10))

        vectors_in = sem("vectors_in")
        weights_in = sem("weights_in")
        experts_in = sem("experts_in")
        x_in = [sem(f"x_in{b}") for b in range(B)]
        setup_done = sem("setup_done")
        root_ready = sem("root_ready")
        var_ready = sem("var_ready")
        std_ready = sem("std_ready")
        angle_ready = sem("angle_ready")
        sine_ready = sem("sine_ready")
        dve_chain = sem("dve_chain")
        act_chain = sem("act_chain")
        pool_chain = sem("pool_chain")
        xn_ready = sem("xn_ready")
        xp_ready = sem("xp_ready")
        xn_turned = sem("xn_turned")
        xp_turned = sem("xp_turned")
        xnT_ready = sem("xnT_ready")
        xpT_ready = sem("xpT_ready")
        gate_ready = sem("gate_ready")
        q_ready = sem("q_ready")
        k_ready = sem("k_ready")
        v_ready = sem("v_ready")
        gate_read = sem("gate_read")
        q_read = sem("q_read")
        k_read = sem("k_read")
        v_read = sem("v_read")
        mask_ready = sem("mask_ready")
        mask_turned = sem("mask_turned")
        maskT_ready = sem("maskT_ready")
        mask_stored = sem("mask_stored")
        mask_spread = sem("mask_spread")
        parts_ready = sem("parts_ready")
        parts_stored = sem("parts_stored")
        prob_in = sem("prob_in")
        prob_exp = sem("prob_exp")
        hid_ready = sem("hid_ready")
        hid_relu = sem("hid_relu")
        exp_done = sem("exp_done")
        exp_read = sem("exp_read")
        acc_ready = sem("acc_ready")
        acc_turned = sem("acc_turned")
        base_ready = sem("base_ready")
        rows_set = sem("rows_set")
        ones_set = sem("ones_set")
        unit_in = sem("unit_in")
        item_ready = sem("item_ready")
        item_read = sem("item_read")
        max_ready = sem("max_ready")
        max_turned = sem("max_turned")
        maxT_ready = sem("maxT_ready")
        maxT_parts = sem("maxT_parts")
        max_in = sem("max_in")
        logits_ready = sem("logits_ready")
        exp_out = sem("exp_out")
        v_staged = sem("v_staged")
        av_done = sem("av_done")
        sums_out = sem("sums_out")
        sums_stored = sem("sums_stored")
        sums_in = sem("sums_in")
        outT_ready = sem("outT_ready")
        proj_ready = sem("proj_ready")
        row_var = sem("row_var")
        row_std = sem("row_std")
        result_ready = sem("result_ready")
        tail_chain = sem("tail_chain")
        result_out = sem("result_out")

        def two_banks(i):
            return bank[:, i:i + 2, :].rearrange("p c s -> p (c s)")

        with ExitStack() as one:
            wq, wk, wv = (sb(one, n, [P, D]) for n in ("wq", "wk", "wv"))
            gw = sb(one, "gw", [P, E])
            gb_row = sb(one, "gb_row", [P, E])
            bv_row = sb(one, "bv_row", [P, D])
            bqk = sb(one, "bqk", [P, 2])
            W1 = sb(one, "W1", [P, E, F])
            W2 = sb(one, "W2", [P, E, FT, D])
            B1 = sb(one, "B1", [P, E, FT])
            B2 = sb(one, "B2", [P, E])
            rden = sb(one, "rden", [P, D // 2])
            posc = sb(one, "posc", [P, NT])
            ang = sb(one, "ang", [P, NT, D // 2])
            turns_ = sb(one, "turns_", [P, NT, D // 2])
            half_sin = sb(one, "half_sin", [P, NT, D // 2])
            pe_ = sb(one, "pe_", [P, NT, D])
            stat = sb(one, "stat", [P, 4, B * NT])
            mean, var, std, rstd = (stat[:, i, :] for i in range(4))
            xc = sb(one, "xc", [P, NT, D])
            xs = sb(one, "xs", [P, NT, D])
            xnT = sb(one, "xnT", [P, S])
            xpT = sb(one, "xpT", [P, S])
            q32 = sb(one, "q32", [P, S])
            k32 = sb(one, "k32", [P, S])
            parts = sb(one, "parts", [P, 2, PARTS, S], BF16)
            gate = sb(one, "gate", [P, 8, NT, E])
            few = sb(one, "few", [P, 8, NT])
            order = sb(one, "order", [P, E])
            mask = sb(one, "mask", [P, NT, E])
            maskT = sb(one, "maskT", [E, S], BF16)
            mask_all = sb(one, "mask_all", [P, E, S], BF16)
            hid = sb(one, "hid", [P, 2, FT, CH])
            masked = sb(one, "masked", [P, CH])
            acc = sb(one, "acc", [P, CH])

            def tiles(t, b):
                return t[:, bass.ds(b * NT, NT), :]

            def spread(t):
                return t.unsqueeze(2).to_broadcast([P, NT, E])

            ranks = order[:].unsqueeze(1).to_broadcast([P, NT, E])

            with nc.Block() as block:
                @block.sync
                def _(sp):
                    xv = x.rearrange("b (t p) d -> p (b t) d", p=P)
                    for b in range(B):
                        sp.dma_start(X[:, b * NT:(b + 1) * NT, :], xv[:, b * NT:(b + 1) * NT, :]).then_inc(x_in[b], 16)
                    for dst, src in ((coef[:, 0:3], row(rby)), (rden[:], row(freq)), (posc[:], pos),
                                     (gam_row[:], row(gamma)), (beta_row[:], row(beta)), (bo_row[:], row(bo)),
                                     (bv_row[:], row(bv)), (gb_row[:], row(gate_b)), (order[:], row(rank_in)),
                                     (bqk[:, 0:1], bq), (bqk[:, 1:2], bk)):
                        sp.dma_start(dst, src).then_inc(vectors_in, 16)
                    for dst, src in ((ident[:], ident_in), (wq[:], wqT), (wk[:], wkT), (wv[:], wvT), (gw[:], gate_w),
                                     (wo[:], woT)):
                        sp.dma_start(dst, src).then_inc(weights_in, 16)
                    for dst, src in ((W1[:], w1.rearrange("e d f -> d e f")), (B1[:], b1T), (B2[:], b2T),
                                     (W2[:], w2.rearrange("e (t p) d -> p e t d", p=P))):
                        sp.dma_start(dst, src).then_inc(experts_in, 16)
                    with sp.Fori(0, B) as b:
                        sp.wait_ge(maskT_ready, b + 1)
                        sp.dma_start(mask_rows[bass.ds(b, 1)].rearrange("o e s -> (o e) s"),
                                     maskT[:]).then_inc(mask_stored, 16)
                        sp.wait_ge(mask_stored, b * 16 + 16)
                        sp.dma_start(mask_all[:].rearrange("p e s -> p (e s)"),
                                     mask_rows[bass.ds(b, 1)].rearrange("o e s -> (o e s)").partition_broadcast(P)
                                     ).then_inc(mask_spread, 16)
                        for m in range(2):
                            sp.wait_ge(parts_ready, b * 2 + m + 1)
                            for n in range(PARTS):
                                for g in range(NG):
                                    rows = slice(g * U * DK, (g + 1) * U * DK)
                                    sp.dma_start(qk_parts[m, bass.ds(b * NG + g, 1), n].rearrange("o d u s -> u (o d) s"),
                                                 parts[rows, m, n, :]).then_inc(parts_stored, 16)
                    sp.wait_ge(parts_stored, (B + 1) * PARTS_STORES)

                @block.scalar
                def _(act):
                    act.wait_ge(setup_done, 1)
                    nc.scalar.activation(ROOT, DEN2, ACT.Sqrt).then_inc(root_ready, 1)
                    act.wait_ge(var_ready, 1)
                    nc.scalar.activation(std, var, ACT.Sqrt).then_inc(std_ready, 1)
                    act.wait_ge(angle_ready, 1)
                    nc.scalar.activation(pe_[:, :, 0:D:2], ang[:], ACT.Sin).then_inc(sine_ready, 1)
                    nc.scalar.activation(half_sin[:], ang[:], ACT.Sin, scale=0.5).then_inc(sine_ready, 1)
                    with act.Fori(0, B) as b:
                        act.wait_ge(xp_turned, b + 1)
                        nc.scalar.copy(xpT[:], two_banks(6)).then_inc(xpT_ready, 1)
                        act.wait_ge(prob_in, b + 1)
                        nc.scalar.activation(gate[:, 2], gate[:, 1], ACT.Exp).then_inc(prob_exp, 1)
                        act.wait_ge(k_ready, b + 1)
                        nc.scalar.activation(k32[:], two_banks(0), ACT.Identity, bias=bqk[:, 1:2]).then_inc(k_read, 1)
                        with act.Fori(0, NC) as c:
                            for e in range(E):
                                for t in range(FT):
                                    j = b * (NC * E * FT) + c * (E * FT) + (e * FT + t)
                                    act.wait_ge(hid_ready, j + 1)
                                    nc.scalar.activation(hid[:, e % 2, t, :], bank[:, t % 2, :], ACT.Relu,
                                                         bias=B1[:, e, t:t + 1]).then_inc(hid_relu, 1)

                @block.vector
                def _(dve):
                    v = nc.vector
                    ch = Chain(dve, dve_chain)
                    dve.wait_ge(vectors_in, 11 * 16)
                    v.tensor_scalar(OUT_FACTOR, YELLOW, EPS_ADAPTIVE, 1.0, ALU.mult, ALU.add)
                    v.tensor_scalar(LN_EPS, BLUE, 0.1, 1.0, ALU.mult, ALU.add)
                    v.tensor_scalar(QSCALE, RED, 0.1, 1.0, ALU.mult, ALU.add)
                    v.tensor_scalar(GAM, RED, 0.1, 1.0, ALU.mult, ALU.add)
                    v.tensor_scalar(TMP, YELLOW, PHASE, 1.0, ALU.mult, ALU.add)
                    ch.link(v.tensor_scalar(DEN2, RED, TENSION, 1.0, ALU.mult, ALU.add))
                    v.tensor_scalar(LN_EPS, LN_EPS, 1e-5, None, ALU.mult)
                    v.scalar_tensor_tensor(QSCALE, BLUE, 0.05, QSCALE, ALU.mult, ALU.add)
                    v.scalar_tensor_tensor(GAM, YELLOW, 0.05, GAM, ALU.mult, ALU.add)
                    v.tensor_scalar(rden[:], rden[:], TMP, None, ALU.mult)
                    v.tensor_scalar(DEN2, DEN2, float(DK), None, ALU.mult).then_inc(setup_done, 1)
                    ch.link(v.memset(few[:, 7], 0.0))
                    v.memset(few[:, 6], 0.0).then_inc(parts_stored, PARTS_STORES)
                    v.scalar_tensor_tensor(QSCALE, YELLOW, 0.15, QSCALE, ALU.mult, ALU.add)
                    v.tensor_scalar(gam_row[:], gam_row[:], GAM, None, ALU.mult)
                    ch.link(v.reciprocal(rden[:], rden[:]))
                    ch.link(v.tensor_tensor(ang[:], posc[:].unsqueeze(2).to_broadcast([P, NT, D // 2]),
                                            rden[:].unsqueeze(1).to_broadcast([P, NT, D // 2]), ALU.mult))
                    ch.link(v.tensor_scalar(turns_[:], ang[:], 0.5 / PI, ROUND, ALU.mult, ALU.add))
                    ch.link(v.tensor_scalar(turns_[:], turns_[:], ROUND, None, ALU.subtract))
                    ch.link(v.scalar_tensor_tensor(ang[:], turns_[:], -TWO_PI_HI, ang[:], ALU.mult, ALU.add))
                    ch.link(v.scalar_tensor_tensor(ang[:], turns_[:], -TWO_PI_LO, ang[:], ALU.mult, ALU.add))
                    v.tensor_scalar(ang[:], ang[:], -PI_DOWN, PI_DOWN, ALU.max, ALU.min).then_inc(angle_ready, 1)
                    dve.wait_ge(root_ready, 1)
                    ch.link(v.reciprocal(TMP, ROOT))
                    ch.link(v.scalar_tensor_tensor(TMP, TMP, DEN2, ROOT, ALU.mult, ALU.add))
                    ch.link(v.tensor_scalar(TMP, TMP, 0.5, None, ALU.mult))
                    ch.link(v.reciprocal(TMP, TMP))
                    ch.link(v.tensor_scalar(QSCALE, QSCALE, TMP, None, ALU.mult))

                    for b in range(B):
                        sl = slice(b * NT, (b + 1) * NT)
                        dve.wait_ge(x_in[b], 16)
                        ch.link(v.tensor_reduce(mean[:, sl], X[:, sl, :], AX_X, ALU.add))
                        ch.link(v.tensor_scalar(mean[:, sl], mean[:, sl], 1.0 / D, None, ALU.mult))
                        ch.link(v.tensor_tensor(xc[:], X[:, sl, :], mean[:, sl].unsqueeze(2).to_broadcast([P, NT, D]),
                                                ALU.subtract))
                        ch.link(v.tensor_tensor(xs[:], xc[:], xc[:], ALU.mult))
                        ch.link(v.tensor_reduce(var[:, sl], xs[:], AX_X, ALU.add))
                    v.tensor_scalar(var, var, 1.0 / D, 1e-5, ALU.mult, ALU.add).then_inc(var_ready, 1)
                    dve.wait_ge(sine_ready, 2)
                    ch.link(v.tensor_tensor(half_sin[:], half_sin[:], half_sin[:], ALU.mult))
                    ch.link(v.tensor_scalar(pe_[:, :, 1:D:2], half_sin[:], -2.0, 1.0, ALU.mult, ALU.add))
                    dve.wait_ge(std_ready, 1)
                    ch.link(v.reciprocal(rstd, std))
                    ch.link(v.tensor_tensor(rstd, rstd, var, ALU.mult))
                    ch.link(v.tensor_tensor(rstd, rstd, std, ALU.add))
                    ch.link(v.tensor_scalar(rstd, rstd, 0.5, None, ALU.mult))
                    ch.link(v.reciprocal(rstd, rstd))

                    with dve.Fori(0, B) as b:
                        ch.turn(b, FRONT_STEPS)
                        ch.link(v.tensor_tensor(xc[:], tiles(X, b), stat[:, 0, bass.ds(b * NT, NT)].unsqueeze(2)
                                                .to_broadcast([P, NT, D]), ALU.subtract))
                        v.tensor_tensor(xc[:], xc[:], stat[:, 3, bass.ds(b * NT, NT)].unsqueeze(2)
                                        .to_broadcast([P, NT, D]), ALU.mult).then_inc(xn_ready, 1)
                        dve.wait_ge(xn_ready, b + 1)
                        v.tensor_tensor(xs[:], xc[:], pe_[:], ALU.add).then_inc(xp_ready, 1)
                        v.tensor_tensor(tiles(XP, b), xc[:], pe_[:], ALU.add)
                        dve.wait_ge(xn_turned, b + 1)
                        v.tensor_copy(xnT[:], two_banks(4)).then_inc(xnT_ready, 1)
                        dve.wait_ge(q_ready, b + 1)
                        ch.done(v.tensor_scalar(q32[:], two_banks(6), bqk[:, 0:1], QSCALE, ALU.add, ALU.mult))
                        dve.wait_ge(gate_ready, b + 1)
                        ch.link(v.tensor_tensor(gate[:, 0], bank[:, 4, 0:NT * E].rearrange("p (t e) -> p t e", e=E),
                                                gb_row[:].unsqueeze(1).to_broadcast([P, NT, E]), ALU.add))
                        ch.link(v.tensor_reduce(few[:, 0], gate[:, 0], AX_X, ALU.max))
                        v.tensor_tensor(gate[:, 1], gate[:, 0], spread(few[:, 0]), ALU.subtract).then_inc(prob_in, 1)
                        dve.wait_ge(v_ready, b + 1)
                        v.tensor_tensor(tiles(V, b), two_banks(2).rearrange("p (t d) -> p t d", d=D),
                                        bv_row[:].unsqueeze(1).to_broadcast([P, NT, D]), ALU.add).then_inc(v_read, 1)
                        dve.wait_ge(prob_exp, b + 1)
                        ch.link(v.tensor_reduce(few[:, 1], gate[:, 2], AX_X, ALU.add))
                        ch.link(v.reciprocal(few[:, 1], few[:, 1]))
                        ch.link(v.tensor_tensor(gate[:, 3], gate[:, 2], spread(few[:, 1]), ALU.mult))
                        ch.link(v.tensor_reduce(few[:, 2], gate[:, 3], AX_X, ALU.max))
                        ch.link(v.tensor_tensor(gate[:, 4], gate[:, 3], spread(few[:, 2]), ALU.is_equal))
                        ch.link(v.tensor_tensor(gate[:, 4], gate[:, 4], ranks, ALU.mult))
                        ch.link(v.tensor_reduce(few[:, 3], gate[:, 4], AX_X, ALU.max))
                        ch.link(v.tensor_tensor(gate[:, 5], ranks, spread(few[:, 3]), ALU.is_equal))
                        ch.link(v.scalar_tensor_tensor(gate[:, 3], gate[:, 5], -2.0, gate[:, 3], ALU.mult, ALU.add))
                        ch.link(v.tensor_reduce(few[:, 4], gate[:, 3], AX_X, ALU.max))
                        ch.link(v.tensor_tensor(gate[:, 4], gate[:, 3], spread(few[:, 4]), ALU.is_equal))
                        ch.link(v.tensor_tensor(gate[:, 4], gate[:, 4], ranks, ALU.mult))
                        ch.link(v.tensor_reduce(few[:, 5], gate[:, 4], AX_X, ALU.max))
                        ch.link(v.tensor_tensor(gate[:, 6], ranks, spread(few[:, 5]), ALU.is_equal))
                        v.tensor_tensor(mask[:], gate[:, 5], gate[:, 6], ALU.add).then_inc(mask_ready, 1)
                        dve.wait_ge(k_read, b + 1)
                        dve.wait_ge(parts_stored, b * PARTS_STORES + PARTS_STORES)
                        for m, t32 in ((0, q32), (1, k32)):
                            ch.link(v.tensor_copy(parts[:, m, 0, :], t32[:]))
                            ch.link(v.tensor_tensor(t32[:], t32[:], parts[:, m, 0, :], ALU.subtract))
                            ch.link(v.tensor_copy(parts[:, m, 1, :], t32[:]))
                            v.tensor_tensor(parts[:, m, 2, :], t32[:], parts[:, m, 1, :],
                                            ALU.subtract).then_inc(parts_ready, 1)
                            if m == 0:
                                dve.wait_ge(mask_turned, b + 1)
                                v.tensor_copy(maskT[:], bank[0:E, 4:6, :].rearrange("p c s -> p (c s)")
                                              ).then_inc(maskT_ready, 1)
                        with dve.Fori(0, NC) as c:
                            ch.turn(c, CHUNK_STEPS)
                            for e in range(E):
                                n = b * (NC * E) + c * E + e
                                dve.wait_ge(exp_done, n + 1)
                                if e == 0:
                                    dve.wait_ge(mask_spread, b * 16 + 16)
                                dst = acc if e == 0 else masked
                                ins = v.scalar_tensor_tensor(dst[:], bank[:, 2 + e % 2, :], B2[:, e:e + 1],
                                                             mask_all[:, e, bass.ds(c * CH, CH)], ALU.add, ALU.mult)
                                ins.then_inc(exp_read, 1)
                                dve.wait_ge(exp_read, n + 1)
                                if 0 < e < E - 1:
                                    ch.link(v.tensor_tensor(acc[:], acc[:], masked[:], ALU.add))
                            v.tensor_tensor(acc[:], acc[:], masked[:], ALU.add).then_inc(acc_ready, 1)
                            dve.wait_ge(acc_turned, b * NC + c + 1)
                            xt = X[:, bass.ds(b * NT + c * (NT // NC), NT // NC), :]
                            v.tensor_tensor(xt, xt, bank[:, 5, :].rearrange("p (t d) -> p t d", d=D),
                                            ALU.add).then_inc(base_ready, 1)
                            ch.end_turns(NC)
                        ch.end_turns(B)

                @block.tensor
                def _(pe):
                    mm, turned = nc.tensor.matmul, nc.tensor.transpose
                    pe.wait_ge(weights_in, 6 * 16)
                    pe.wait_ge(experts_in, 4 * 16)
                    with pe.Fori(0, B) as b:
                        pe.wait_ge(xn_ready, b + 1)
                        for t in range(NT):
                            last = turned(bank[:, 4 + t // 4, (t % 4) * P:(t % 4 + 1) * P], xc[:, t, :], ident[:])
                        last.then_inc(xn_turned, 1)
                        pe.wait_ge(xp_ready, b + 1)
                        for t in range(NT):
                            last = turned(bank[:, 6 + t // 4, (t % 4) * P:(t % 4 + 1) * P], xs[:, t, :], ident[:])
                        last.then_inc(xp_turned, 1)
                        pe.wait_ge(xnT_ready, b + 1)
                        for t in range(NT):
                            last = mm(bank[:, 4, t * E:(t + 1) * E], xnT[:, t * P:(t + 1) * P], gw[:], start=True, stop=True)
                        last.then_inc(gate_ready, 1)
                        pe.wait_ge(xpT_ready, b + 1)
                        for c in range(NC):
                            last = mm(bank[:, 6 + c, :], wq[:], xpT[:, c * CH:(c + 1) * CH], start=True, stop=True)
                        last.then_inc(q_ready, 1)
                        for c in range(NC):
                            last = mm(bank[:, c, :], wk[:], xpT[:, c * CH:(c + 1) * CH], start=True, stop=True)
                        last.then_inc(k_ready, 1)
                        for t in range(NT):
                            last = mm(bank[:, 2 + t // 4, (t % 4) * P:(t % 4 + 1) * P], xpT[:, t * P:(t + 1) * P], wv[:],
                                      start=True, stop=True)
                        last.then_inc(v_ready, 1)
                        pe.wait_ge(mask_ready, b + 1)
                        for t in range(NT):
                            last = turned(bank[0:E, 4 + t // 4, (t % 4) * P:(t % 4 + 1) * P], mask[:, t, :], ident[:])
                        last.then_inc(mask_turned, 1)
                        with pe.Fori(0, NC) as c:
                            pe.wait_ge(k_read, b + 1)
                            pe.wait_ge(v_read, b + 1)
                            def second(e, t):
                                if t == 0 and e >= 2:
                                    pe.wait_ge(exp_read, b * (NC * E) + c * E + e - 1)
                                pe.wait_ge(hid_relu, b * (NC * E * FT) + c * (E * FT) + (e * FT + t + 1))
                                last = mm(bank[:, 2 + e % 2, :], W2[:, e, t, :], hid[:, e % 2, t, :],
                                          start=(t == 0), stop=(t == FT - 1))
                                if t == FT - 1:
                                    last.then_inc(exp_done, 1)

                            for e in range(E):
                                for t in range(FT):
                                    if e or t >= 2:
                                        pe.wait_ge(hid_relu, b * (NC * E * FT) + c * (E * FT) + (e * FT + t - 1))
                                    mm(bank[:, t % 2, :], W1[:, e, t * P:(t + 1) * P], xnT[:, bass.ds(c * CH, CH)],
                                       start=True, stop=True).then_inc(hid_ready, 1)
                                    if e:
                                        second(e - 1, t)
                            for t in range(FT):
                                second(E - 1, t)
                            pe.wait_ge(acc_ready, b * NC + c + 1)
                            for t in range(NT // NC):
                                last = turned(bank[:, 5, t * P:(t + 1) * P], acc[:, t * P:(t + 1) * P], ident[:])
                            last.then_inc(acc_turned, 1)

        STEPS = NT
        CREDIT_AV, CREDIT_EXP, CREDIT_ITEM, CREDIT_PAIR = STEPS, 2, 2, 1
        CREDIT_MAX, CREDIT_SUMS = PARTS * 16, 2 * U * 16
        UC = U * S
        LOADS = 2 * PARTS
        CREDIT_UNIT = LOADS * 16
        with ExitStack() as two:
            QS = sb(two, "QS", [KR2, RING * UC], BF16)
            KS = sb(two, "KS", [KR2, RING * UC], BF16)
            probs = sb(two, "probs", [P, 2, U, CH])
            VS = sb(two, "VS", [P, STEPS, U, 32])
            row_max = sb(two, "row_max", [P, ITEMS])
            neg_max = sb(two, "neg_max", [P, ITEMS])
            maxT = sb(two, "maxT", [ITEMS, P])
            zeros = sb(two, "zeros", [ITEMS, P])
            max_rest = sb(two, "max_rest", [ITEMS, P])
            max_parts = sb(two, "max_parts", [ITEMS, PARTS, P], BF16)
            sums = sb(two, "sums", [P, 2, CH])

            with nc.Block() as block:
                @block.sync
                def _(sp):
                    def ahead(*values):
                        for value in values:
                            if not isinstance(value, int):
                                sp.compute_val(value)

                    def load_unit(u):
                        slot = u & (RING - 1)
                        ahead(slot)
                        cols = bass.ds(slot * UC, UC)
                        sp.wait_ge(unit_in, u * (LOADS * 16) + CREDIT_UNIT)
                        for i in range(PARTS):
                            rows = slice(i * PARTS * DK, (i + 1) * PARTS * DK)
                            sp.dma_start(KS[rows, cols], qk_parts[1, bass.ds(u, 1)].rearrange(
                                "o n d u s -> (o n d) (u s)")).then_inc(unit_in, 16)
                            q = qk_parts[0, bass.ds(u, 1), i].rearrange("o d u s -> (o d) (u s)")
                            sp.dma_start(QS[rows, cols], q.unsqueeze(0).to_broadcast([PARTS, DK, UC])).then_inc(unit_in, 16)

                    def load_max(v):
                        slot = v & (2 * RING - 1)
                        ahead(slot)
                        sp.wait_ge(maxT_parts, v + 2)
                        sp.wait_ge(max_in, v * (PARTS * 16) + CREDIT_MAX)
                        for n in range(PARTS):
                            sp.dma_start(QS[KR + n:KR + n + 1, bass.ds(slot * HALF, HALF)],
                                         max_parts[:, n, :]).then_inc(max_in, 16)

                    def store_sums(w):
                        b, g, c = (w >> 3) & (B - 1), (w >> 1) & (NG - 1), w & (NC - 1)
                        ahead(b, g, c)
                        sp.wait_ge(sums_out, w + 1 + CREDIT_PAIR)
                        sp.wait_ge(sums_stored, w * (U * 16) + CREDIT_SUMS)
                        for u in range(U):
                            dst = attn_sums[:, bass.ds(b, 1), bass.ds(g * (U * DK) + u * DK, DK), bass.ds(c * CH, CH)]
                            sp.dma_start(dst.rearrange("m o d q -> (m o) d q"),
                                         sums[32 * u:32 * u + 2 * DK, bass.ds(c, 1), :]).then_inc(sums_stored, 16)

                    sp.wait_ge(rows_set, 2)
                    with sp.Fori(0, RING) as u:
                        load_unit(u)
                    with sp.Fori(0, LEAD) as v:
                        load_max(v)
                    load_max(LEAD)
                    with sp.Fori(0, NU - RING) as u:
                        store_sums(2 * u)
                        load_max(2 * u + (LEAD + 1))
                        store_sums(2 * u + 1)
                        ahead((u + RING) & (RING - 1))
                        sp.wait_ge(av_done, u * (NC * STEPS) + (NC * STEPS + CREDIT_AV))
                        load_unit(u + RING)
                        load_max(2 * u + (LEAD + 2))
                    with sp.Fori(2 * (NU - RING), NW - LEAD - 1) as w:
                        store_sums(w)
                        load_max(w + (LEAD + 1))
                    with sp.Fori(NW - LEAD - 1, NW) as w:
                        store_sums(w)
                    sp.wait_ge(sums_stored, NW * (U * 16) + CREDIT_SUMS)

                @block.tensor
                def _(pe):
                    mm = nc.tensor.matmul

                    def max_item(i, v):
                        if i == 0:
                            pe.wait_ge(unit_in, (v >> 1) * (LOADS * 16) + (LOADS * 16 + CREDIT_UNIT))
                        pe.wait_ge(item_read, v * ITEMS + (i - 1 + CREDIT_ITEM))
                        head, tile = i // NT, i % NT
                        at = (v & 7) * HALF + head * S
                        for c in range(NC):
                            last = mm(bank[:, 2 * (i % 2) + c, :], QS[0:KR, bass.ds(at + tile * P, P)],
                                      KS[0:KR, bass.ds(at + c * CH, CH)], start=True, stop=True)
                        last.then_inc(item_ready, 1)

                    def turn_max(v):
                        pe.wait_ge(max_ready, v + 1)
                        nc.tensor.transpose(bank[0:ITEMS, 7, 0:P], neg_max[:], ident[:]).then_inc(max_turned, 1)

                    def logits(w, t, u):
                        if t == 0 and u == 0:
                            pe.wait_ge(max_in, (w >> 1) * (2 * PARTS * 16) + (2 * PARTS * 16 + CREDIT_MAX))
                        pe.wait_ge(exp_out, w * (STEPS * U) + (t * U + u - 1 + CREDIT_EXP))
                        at = ((w >> 1) & (RING - 1)) * UC + u * S
                        mm(bank[:, 4 + u % 2, :], KS[:, bass.ds(at + t * P, P)],
                           QS[:, bass.ds(at + (w & 1) * CH, CH)], start=True, stop=True).then_inc(logits_ready, 1)

                    def product(w, t):
                        if t == 0:
                            pe.wait_ge(sums_out, w + CREDIT_PAIR)
                        pe.wait_ge(v_staged, (w >> 1) * STEPS + (t + 1))
                        pe.wait_ge(exp_out, w * (STEPS * U) + (t * U + U + CREDIT_EXP))
                        for u in range(U):
                            last = mm(bank[32 * u:32 * u + 32, 6, :], VS[:, t, u, :], probs[:, t % 2, u, :],
                                      start=(t == 0), stop=(t == STEPS - 1))
                        last.then_inc(av_done, 1)

                    def pair(w, items=True, turn=True, before=True):
                        for t in range(STEPS):
                            logits(w, t, 0)
                            logits(w, t, 1)
                            if t:
                                product(w, t - 1)
                            elif before:
                                product(w - 1, STEPS - 1)
                            logits(w, t, 2)
                            logits(w, t, 3)
                            if turn and t == 1:
                                turn_max(w + (LEAD - 1))
                            if items:
                                max_item(2 * t, w + LEAD)
                                max_item(2 * t + 1, w + LEAD)

                    pe.wait_ge(rows_set, 3)
                    for i in range(ITEMS):
                        max_item(i, 0)
                    with pe.Fori(1, LEAD) as v:
                        for i in range(ITEMS):
                            max_item(i, v)
                            if i == 3:
                                turn_max(v - 1)
                    pair(0, before=False)
                    with pe.Fori(1, NW - LEAD) as w:
                        pair(w)
                    pair(NW - LEAD, items=False)
                    with pe.Fori(NW - LEAD + 1, NW) as w:
                        pair(w, items=False, turn=False)
                    product(NW - 1, STEPS - 1)

                @block.scalar
                def _(act):
                    with act.Fori(0, NW) as w:
                        for t in range(STEPS):
                            act.wait_ge(av_done, w * STEPS + (t - 1 + CREDIT_AV))
                            for u in range(U):
                                act.wait_ge(logits_ready, w * (STEPS * U) + (t * U + u + 1))
                                nc.scalar.activation(probs[:, t % 2, u, :], bank[:, 4 + u % 2, :],
                                                     ACT.Exp).then_inc(exp_out, 1)

                @block.vector
                def _(dve):
                    v_ = nc.vector
                    v_.memset(QS[64:KR, :], 0.0).then_inc(rows_set, 1)
                    v_.memset(KS[64:KR, :], 0.0).then_inc(rows_set, 1)
                    v_.memset(KS[KR:KR2, :], 1.0).then_inc(rows_set, 1)
                    v_.memset(row_max[:, 0:1], 0.0).then_inc(item_read, CREDIT_ITEM)
                    v_.memset(row_max[:, 1:2], 0.0).then_inc(exp_out, CREDIT_EXP)
                    v_.memset(row_max[:, 2:3], 0.0).then_inc(av_done, CREDIT_AV)
                    v_.memset(row_max[:, 3:4], 0.0).then_inc(sums_stored, CREDIT_SUMS)
                    v_.memset(row_max[:, 4:5], 0.0).then_inc(max_in, CREDIT_MAX)
                    v_.memset(row_max[:, 7:8], 0.0).then_inc(unit_in, CREDIT_UNIT)
                    v_.memset(row_max[:, 5:6], 0.0).then_inc(sums_out, CREDIT_PAIR)
                    v_.memset(row_max[:, 6:7], 0.0).then_inc(maxT_parts, 1)

                    def reduce_item(i, v):
                        dve.wait_ge(item_ready, v * ITEMS + (i + 1))
                        v_.tensor_reduce(row_max[:, i:i + 1], two_banks(2 * (i % 2)), AX_X,
                                         ALU.max).then_inc(item_read, 1)

                    def negate(v):
                        dve.wait_ge(item_read, v * ITEMS + (ITEMS + CREDIT_ITEM))
                        v_.tensor_scalar(neg_max[:], row_max[:], -1.0, None, ALU.mult).then_inc(max_ready, 1)
                        dve.wait_ge(max_ready, v + 1)

                    def take_turned(v):
                        dve.wait_ge(max_turned, v + 1)
                        dve.wait_ge(maxT_parts, v + 1)
                        v_.tensor_copy(maxT[:], bank[0:ITEMS, 7, 0:P]).then_inc(maxT_ready, 1)

                    def take_sums(w):
                        dve.wait_ge(av_done, w * STEPS + (STEPS + CREDIT_AV))
                        dve.wait_ge(sums_stored, w * (U * 16) + CREDIT_SUMS - U * 16)
                        v_.tensor_copy(sums[:, bass.ds(w & 1, 1), :].rearrange("p o q -> p (o q)"),
                                       bank[:, 6, :]).then_inc(sums_out, 1)

                    def pair(w, items=True, turn=True, before=True):
                        if before:
                            take_sums(w - 1)
                        for t in range(STEPS):
                            if items:
                                reduce_item(2 * t, w + LEAD)
                            if turn and t == 2:
                                take_turned(w + (LEAD - 1))
                            if items:
                                reduce_item(2 * t + 1, w + LEAD)
                        if items:
                            negate(w + LEAD)

                    for i in range(ITEMS):
                        reduce_item(i, 0)
                    negate(0)
                    with dve.Fori(1, LEAD) as v:
                        for i in range(ITEMS):
                            reduce_item(i, v)
                            if i == 4:
                                take_turned(v - 1)
                        negate(v)
                    pair(0, before=False)
                    with dve.Fori(1, NW - LEAD) as w:
                        pair(w)
                    pair(NW - LEAD, items=False)
                    with dve.Fori(NW - LEAD, NW) as w:
                        take_sums(w)

                @block.gpsimd
                def _(pool):
                    ch = Chain(pool, pool_chain)

                    def stage_v(u, t):
                        pool.wait_ge(av_done, u * (NC * STEPS) + (t + 1))
                        pool.wait_ge(ones_set, 1)
                        at = bass.ds(((u >> 2) & (B - 1)) * NT + t, 1)
                        nc.gpsimd.tensor_copy(VS[:, t, :, 0:DK],
                                              V[:, at, bass.ds((u & (NG - 1)) * (U * DK), U * DK)].rearrange(
                                                  "p o (u d) -> p (o u) d", d=DK)).then_inc(v_staged, 1)

                    def split_max(v):
                        pool.wait_ge(maxT_ready, v + 1)
                        pool.wait_ge(max_in, v * (PARTS * 16) + CREDIT_MAX)
                        pool.wait_ge(ones_set, 1)
                        ch.link(nc.gpsimd.tensor_tensor(max_parts[:, 0, :], maxT[:], zeros[:], ALU.add))
                        ch.link(nc.gpsimd.tensor_tensor(max_rest[:], maxT[:], max_parts[:, 0, :], ALU.subtract))
                        ch.link(nc.gpsimd.tensor_tensor(max_parts[:, 1, :], max_rest[:], zeros[:], ALU.add))
                        nc.gpsimd.tensor_tensor(max_parts[:, 2, :], max_rest[:], max_parts[:, 1, :],
                                                ALU.subtract).then_inc(maxT_parts, 1)

                    nc.gpsimd.memset(zeros[:], 0.0)
                    nc.gpsimd.memset(VS[:], 1.0).then_inc(ones_set, 1)
                    for t in range(STEPS):
                        stage_v(0, t)
                    split_max(0)
                    split_max(1)
                    with pool.Fori(0, NU - 1) as u:
                        ch.turn(u, 2 * 3)
                        split_max(2 * u + 2)
                        stage_v(u + 1, 0)
                        stage_v(u + 1, 1)
                        split_max(2 * u + 3)
                        for t in range(2, STEPS):
                            stage_v(u + 1, t)
                        ch.end_turns(NU - 1)

        with ExitStack() as three:
            numer = sb(three, "numer", [P, 2, S])
            denom = sb(three, "denom", [P, 2, S])
            outT = sb(three, "outT", [P, S])
            y = sb(three, "y", [P, NT, D])
            ysq = sb(three, "ysq", [P, NT, D])
            result = sb(three, "result", [P, 2, NT, D])
            m8, v8, s8, r8 = (sb(three, n, [P, NT]) for n in ("m8", "v8", "s8", "r8"))

            with nc.Block() as block:
                @block.sync
                def _(sp):
                    ov = out.rearrange("b (t p) d -> b p t d", p=P)

                    def load(b):
                        for m, dst in ((0, numer), (1, denom)):
                            sp.dma_start(dst[:, bass.ds(b & 1, 1), :].rearrange("p o s -> p (o s)"),
                                         attn_sums[m, bass.ds(b, 1)].rearrange("o p s -> (o p) s")).then_inc(sums_in, 16)

                    def store(b):
                        sp.wait_ge(result_ready, b + 1)
                        sp.dma_start(ov[bass.ds(b, 1)].rearrange("o p t d -> p (o t) d"),
                                     result[:, bass.ds(b & 1, 1)].rearrange("p o t d -> p (o t) d")).then_inc(result_out, 16)
                        sp.wait_ge(result_out, b * 16 + 16)

                    load(0)
                    sp.wait_ge(sums_in, 32)
                    load(1)
                    with sp.Fori(0, B - 2) as b:
                        sp.compute_val((b + 2) & 1)
                        store(b)
                        sp.wait_ge(sums_in, b * 32 + 64)
                        load(b + 2)
                    store(B - 2)
                    store(B - 1)

                @block.scalar
                def _(act):
                    with act.Fori(0, B) as b:
                        act.wait_ge(row_var, b + 1)
                        nc.scalar.activation(s8[:], v8[:], ACT.Sqrt).then_inc(row_std, 1)

                @block.tensor
                def _(pe):
                    with pe.Fori(0, B) as b:
                        pe.wait_ge(outT_ready, b + 1)
                        for t in range(NT):
                            last = nc.tensor.matmul(bank[:, t // 4, (t % 4) * P:(t % 4 + 1) * P],
                                                    outT[:, t * P:(t + 1) * P], wo[:], start=True, stop=True)
                        last.then_inc(proj_ready, 1)

                @block.vector
                def _(dve):
                    v = nc.vector
                    ch = Chain(dve, tail_chain)

                    def rows(t):
                        return t[:].unsqueeze(1).to_broadcast([P, NT, D])

                    def spread(t):
                        return t[:].unsqueeze(2).to_broadcast([P, NT, D])

                    with dve.Fori(0, B) as b:
                        ch.turn(b, TAIL_STEPS)
                        tiles = bass.ds(b * NT, NT)
                        dve.wait_ge(sums_in, b * 32 + 32)
                        den = denom[:, bass.ds(b & 1, 1), :].rearrange("p o s -> p (o s)")
                        num = numer[:, bass.ds(b & 1, 1), :].rearrange("p o s -> p (o s)")
                        ch.link(v.reciprocal(den, den))
                        v.scalar_tensor_tensor(outT[:], num, OUT_FACTOR, den, ALU.mult, ALU.mult).then_inc(outT_ready, 1)
                        dve.wait_ge(proj_ready, b + 1)
                        ch.link(v.tensor_tensor(y[:], two_banks(0).rearrange("p (t d) -> p t d", d=D), rows(bo_row),
                                                ALU.add))
                        ch.link(v.tensor_tensor(y[:], y[:], XP[:, tiles, :], ALU.add))
                        ch.link(v.tensor_reduce(m8[:], y[:], AX_X, ALU.add))
                        ch.link(v.tensor_scalar(m8[:], m8[:], 1.0 / D, None, ALU.mult))
                        ch.link(v.tensor_tensor(y[:], y[:], spread(m8), ALU.subtract))
                        ch.link(v.tensor_tensor(ysq[:], y[:], y[:], ALU.mult))
                        ch.link(v.tensor_reduce(v8[:], ysq[:], AX_X, ALU.add))
                        v.tensor_scalar(v8[:], v8[:], 1.0 / D, LN_EPS, ALU.mult, ALU.add).then_inc(row_var, 1)
                        dve.wait_ge(row_std, b + 1)
                        ch.link(v.reciprocal(r8[:], s8[:]))
                        ch.link(v.tensor_tensor(r8[:], r8[:], v8[:], ALU.mult))
                        ch.link(v.tensor_tensor(r8[:], r8[:], s8[:], ALU.add))
                        ch.link(v.tensor_scalar(r8[:], r8[:], 0.5, None, ALU.mult))
                        ch.link(v.reciprocal(r8[:], r8[:]))
                        ch.link(v.tensor_tensor(y[:], y[:], spread(r8), ALU.mult))
                        ch.link(v.tensor_tensor(y[:], y[:], rows(gam_row), ALU.mult))
                        ch.link(v.tensor_tensor(y[:], y[:], rows(beta_row), ALU.add))
                        v.tensor_tensor(result[:, bass.ds(b & 1, 1)].rearrange("p o t d -> p (o t) d"), y[:],
                                        X[:, tiles, :], ALU.add).then_inc(result_ready, 1)
                        ch.end_turns(B)


def kernel(**inputs):
    import numpy as np
    import concourse.bacc as bacc
    from concourse.bass_utils import run_bass_kernel_spmd as run

    def take(name):
        return np.asarray(inputs[name])

    nc = bacc.Bacc("TRN2", target_bir_lowering=False, num_devices=1)
    laid = {
        "x": take("L0_attn_x"), "rby": take("L0_attn_rby"),
        "wqT": take("L0_attn_Wq").T, "bq": take("L0_attn_bq").reshape(P, 1),
        "wkT": take("L0_attn_Wk").T, "bk": take("L0_attn_bk").reshape(P, 1),
        "wvT": take("L0_attn_Wv").T, "bv": take("L0_attn_bv"),
        "woT": take("L0_attn_Wo").T, "bo": take("L0_attn_bo"),
        "gamma": take("L0_attn_ln_gamma"), "beta": take("L0_attn_ln_beta"),
        "gate_w": take("L0_ffn_gate_w"), "gate_b": take("L0_ffn_gate_b"),
        "w1": take("L0_ffn_w1"), "b1T": take("L0_ffn_b1").reshape(E, FT, P).transpose(2, 0, 1),
        "w2": take("L0_ffn_w2"), "b2T": take("L0_ffn_b2").T,
        "ident_in": np.eye(P, dtype=np.float32),
        "freq": np.power(np.float32(10000.0), 2.0 * np.arange(0, D, 2, dtype=np.float32) / np.float32(D)).astype(np.float32),
        "pos": (np.arange(P, dtype=np.float32)[:, None] + np.float32(P) * np.arange(NT, dtype=np.float32)[None, :]),
        "rank_in": np.arange(E, 0, -1).astype(np.float32),
    }
    arrays, args = {}, []
    for name, a in laid.items():
        arrays[f"in_{name}"] = np.ascontiguousarray(a)
        args.append(nc.dram_tensor(f"in_{name}", arrays[f"in_{name}"].shape, mybir.dt.from_np(a.dtype),
                                   kind="ExternalInput").ap())
    out = nc.dram_tensor("out_0", (B, S, D), F32, kind="ExternalOutput").ap()
    build(nc, *args, out)
    return run(nc, [arrays], core_ids=[0]).results[0]["out_0"]
```

```python
from contextlib import ExitStack

import concourse.bass as bass
from concourse import mybir

F32 = mybir.dt.float32
BF16 = mybir.dt.bfloat16
F32R = mybir.dt.float32r
ALU = mybir.AluOpType
ACT = mybir.ActivationFunctionType
AX_X = mybir.AxisListType.X

P = 128
B, S, D = 4, 1024, 128
H, DK = 16, 8
NT = S // P
E, F = 8, 512
FT = F // P
CH = 512
NC = S // CH
U = 4
NG = H // U
NU = B * NG
NW = NU * NC
PARTS = 3
PROD = PARTS * PARTS * DK
KR = 96
KR2 = KR + PARTS
RING = 4
HALF = 2 * S
ITEMS = 16
LEAD = 3
PI = 3.14159265358979
PI_DOWN = 3.1415925
TILES = E * FT
CHUNKS = B * NC
LAG = 2
PARTS_STORES = PARTS * NG * 16
TAIL_STEPS = 16
TENSION = abs(1.0 - 1.0)
PHASE = 0.1
EPS_ADAPTIVE = 0.1 * 1.2246467991473532e-16
ROUND = 1.5 * 2.0 ** 23
TWO_PI_HI = 6.28125
TWO_PI_LO = 6.283185307179586 - 6.28125


class Chain:

    def __init__(self, eng, sem):
        self.eng, self.sem, self.n, self.base, self.outer = eng, sem, 0, 0, []

    def done(self, ins):
        ins.then_inc(self.sem, 1)
        self.n += 1

    def settle(self):
        self.eng.wait_ge(self.sem, self.base + self.n)

    def link(self, ins):
        self.done(ins)
        self.settle()

    def turn(self, i, per_turn):
        self.outer.append((self.base, self.n, per_turn))
        self.base = self.base + i * per_turn

    def end_turns(self, turns):
        self.base, start, per_turn = self.outer.pop()
        assert self.n - start == per_turn, (self.n - start, per_turn)
        self.n = start + turns * per_turn


def row(vec, n=P):
    return vec.partition_broadcast(n)


def build(nc, x, rby, wqT, bq, wkT, bk, wvT, bv, woT, bo, gamma, beta, gate_w, gate_b, w1, b1T, w2, b2T,
          ident_in, freq, pos, rank_in, out):
    with ExitStack() as whole:
        def sb(ctx, name, shape, dt=F32):
            return ctx.enter_context(nc.sbuf_tensor(name, shape, dt))

        def sem(name):
            return whole.enter_context(nc.semaphore(name))

        qk_parts = nc.dram_tensor("qk_parts", (2, NU, PARTS, DK, U, S), BF16, kind="Internal").ap()
        mask_rows = nc.dram_tensor("mask_rows", (B, E, S), BF16, kind="Internal").ap()
        xp_rows = nc.dram_tensor("xp_rows", (B, S, D), F32, kind="Internal").ap()
        attn_sums = nc.dram_tensor("attn_sums", (2, B, P, S), F32, kind="Internal").ap()

        bank = whole.enter_context(nc.psum_tensor("bank", [P, 8, CH], F32))

        X = sb(whole, "X", [P, B * NT, D])
        V = sb(whole, "V", [P, B * NT, D])
        ident = sb(whole, "ident", [P, P])
        wo = sb(whole, "wo", [P, D])
        bo_row = sb(whole, "bo_row", [P, D])
        gam_row = sb(whole, "gam_row", [P, D])
        beta_row = sb(whole, "beta_row", [P, D])
        coef = sb(whole, "coef", [P, 16])
        RED, BLUE, YELLOW, QSCALE, LN_EPS, OUT_FACTOR, DEN2, ROOT, TMP, GAM = (coef[:, i:i + 1] for i in range(10))

        vectors_in = sem("vectors_in")
        weights_in = sem("weights_in")
        experts_in = sem("experts_in")
        x_in = [sem(f"x_in{b}") for b in range(B)]
        setup_done = sem("setup_done")
        q_scaled = sem("q_scaled")
        pe_ready = sem("pe_ready")
        centred = sem("centred")
        root_ready = sem("root_ready")
        var_ready = sem("var_ready")
        std_ready = sem("std_ready")
        angle_ready = sem("angle_ready")
        sine_ready = sem("sine_ready")
        dve_chain = sem("dve_chain")
        act_chain = sem("act_chain")
        pool_chain = sem("pool_chain")
        xn_ready = sem("xn_ready")
        xp_ready = sem("xp_ready")
        xn_turned = sem("xn_turned")
        xp_turned = sem("xp_turned")
        xnT_ready = sem("xnT_ready")
        xpT_ready = sem("xpT_ready")
        gate_ready = sem("gate_ready")
        q_ready = sem("q_ready")
        k_ready = sem("k_ready")
        v_ready = sem("v_ready")
        xn_split = sem("xn_split")
        xp_stored = sem("xp_stored")
        q_read = sem("q_read")
        k_read = sem("k_read")
        v_read = sem("v_read")
        q_rest = sem("q_rest")
        k_rest = sem("k_rest")
        q_second = sem("q_second")
        k_second = sem("k_second")
        q_parts = sem("q_parts")
        k_parts = sem("k_parts")
        q_stored = sem("q_stored")
        k_stored = sem("k_stored")
        mask_ready = sem("mask_ready")
        mask_turned = sem("mask_turned")
        maskT_ready = sem("maskT_ready")
        mask_stored = sem("mask_stored")
        mask_spread = sem("mask_spread")
        prob_in = sem("prob_in")
        prob_exp = sem("prob_exp")
        high_ready = sem("high_ready")
        low_ready = sem("low_ready")
        hid_ready = sem("hid_ready")
        hid_relu = sem("hid_relu")
        hid_split = sem("hid_split")
        hid_used = sem("hid_used")
        sum_read = sem("sum_read")
        acc_ready = sem("acc_ready")
        acc_turned = sem("acc_turned")
        base_ready = sem("base_ready")
        beta_added = sem("beta_added")
        late_in = sem("late_in")
        ones_set = sem("ones_set")
        blank_ready = sem("blank_ready")
        pads_first = sem("pads_first")
        pads_rest = sem("pads_rest")
        unit_in = sem("unit_in")
        item_ready = sem("item_ready")
        item_read = sem("item_read")
        max_ready = sem("max_ready")
        max_turned = sem("max_turned")
        maxT_ready = sem("maxT_ready")
        maxT_parts = sem("maxT_parts")
        max_in = sem("max_in")
        logits_ready = sem("logits_ready")
        exp_out = sem("exp_out")
        v_staged = sem("v_staged")
        av_done = sem("av_done")
        sums_out = sem("sums_out")
        sums_stored = sem("sums_stored")
        sums_in = sem("sums_in")
        outT_ready = sem("outT_ready")
        proj_ready = sem("proj_ready")
        xpb_ready = sem("xpb_ready")
        y_ready = sem("y_ready")
        row_var = sem("row_var")
        row_std = sem("row_std")
        row_scale = sem("row_scale")
        row_norm = sem("row_norm")
        gam_done = sem("gam_done")
        result_ready = sem("result_ready")
        tail_chain = sem("tail_chain")
        result_out = sem("result_out")
        tail_in = [sem(f"tail_in{b}") for b in range(B)]
        tail_xp = [sem(f"tail_xp{b}") for b in range(B)]

        def two_banks(i):
            return bank[:, i:i + 2, :].rearrange("p c s -> p (c s)")

        with ExitStack() as experts:
            W1H = sb(experts, "W1H", [P, E, F], F32R)
            W2H = sb(experts, "W2H", [P, E, F], F32R)
            W1L = sb(experts, "W1L", [P, E, F], F32R)
            W2L = sb(experts, "W2L", [P, E, F], F32R)
            B1 = sb(experts, "B1", [P, E, FT])
            B2 = sb(experts, "B2", [P, E])
            XTH = sb(experts, "XTH", [P, B * S], F32R)
            XTL = sb(experts, "XTL", [P, B * S], F32R)

            with ExitStack() as one:
                wq, wk, wv = (sb(one, n, [P, D]) for n in ("wq", "wk", "wv"))
                gw = sb(one, "gw", [P, E])
                gb_row = sb(one, "gb_row", [P, E])
                bv_row = sb(one, "bv_row", [P, D])
                bqk = sb(one, "bqk", [P, 2])
                rden = sb(one, "rden", [P, D // 2])
                posc = sb(one, "posc", [P, NT])
                ang = sb(one, "ang", [P, NT, D // 2])
                turns_ = sb(one, "turns_", [P, NT, D // 2])
                pe_ = sb(one, "pe_", [P, NT, D])
                bn = sb(one, "bn", [P, B * NT, 6])
                mean_var = sb(one, "mean_var", [P, B * NT, 2])
                stat = sb(one, "stat", [P, 3, B * NT])
                var, std, rstd = (stat[:, i, :] for i in range(3))
                xc = sb(one, "xc", [P, NT, D])
                xs = sb(one, "xs", [P, NT, D])
                xnT = sb(one, "xnT", [P, S])
                xpT = sb(one, "xpT", [P, S])
                q32 = sb(one, "q32", [P, S])
                k32 = sb(one, "k32", [P, S])
                parts = sb(one, "parts", [P, 2, PARTS, S], BF16)
                gate = sb(one, "gate", [P, 8, NT, E])
                few = sb(one, "few", [P, 8, NT])
                order = sb(one, "order", [P, E])
                mask = sb(one, "mask", [P, NT, E])
                maskT = sb(one, "maskT", [E, S], BF16)
                raw = sb(one, "raw", [P, 2, E // B, F])
                half_sin = turns_

                def tiles(t, b):
                    return t[:, bass.ds(b * NT, NT), :]

                def spread(t):
                    return t.unsqueeze(2).to_broadcast([P, NT, E])

                ranks = order[:].unsqueeze(1).to_broadcast([P, NT, E])

                with nc.Block() as block:
                    @block.sync
                    def _(sp):
                        xv = x.rearrange("b (t p) d -> p (b t) d", p=P)
                        for b in range(B):
                            sp.dma_start(X[:, b * NT:(b + 1) * NT, :], xv[:, b * NT:(b + 1) * NT, :]).then_inc(x_in[b], 16)
                        for dst, src in ((ident[:], ident_in), (gw[:], gate_w), (wq[:], wqT), (wk[:], wkT), (wv[:], wvT)):
                            sp.dma_start(dst, src).then_inc(weights_in, 16)
                        for dst, src in ((B1[:], b1T), (B2[:], b2T), (wo[:], woT)):
                            sp.dma_start(dst, src).then_inc(late_in, 16)
                        def move(b, first=False):
                            if not first:
                                sp.wait_ge(low_ready, 2 * b)
                            pair = bass.ds(b * (E // B), E // B)
                            sp.dma_start(raw[:, 0], w1[pair].rearrange("e d f -> d e f")).then_inc(experts_in, 16)
                            for i in range(E // B):
                                sp.dma_start(raw[:, 1, i, :].rearrange("p (t d) -> p t d", d=D),
                                             w2[bass.ds(b * (E // B) + i, 1)].rearrange(
                                                 "o (t p) d -> p (o t) d", p=P)).then_inc(experts_in, 16)
                            sp.wait_ge(xp_ready, b + 1)
                            sp.dma_start(xp_rows[bass.ds(b, 1)].rearrange("o (t p) d -> p (o t) d", p=P),
                                         xs[:]).then_inc(xp_stored, 16)
                            sp.wait_ge(maskT_ready, b + 1)
                            sp.dma_start(mask_rows[bass.ds(b, 1)].rearrange("o e s -> (o e) s"),
                                         maskT[:]).then_inc(mask_stored, 16)
                            for m, ready, stored in ((0, q_parts, q_stored), (1, k_parts, k_stored)):
                                sp.wait_ge(ready, b + 1)
                                for n in range(PARTS):
                                    for g in range(NG):
                                        rows = slice(g * U * DK, (g + 1) * U * DK)
                                        sp.dma_start(qk_parts[m, bass.ds(b * NG + g, 1), n].rearrange(
                                            "o d u s -> u (o d) s"), parts[rows, m, n, :]).then_inc(stored, 16)

                        move(0, first=True)
                        with sp.Fori(1, B) as b:
                            move(b)
                        sp.wait_ge(late_in, 3 * 16)
                        sp.wait_ge(xp_stored, B * 16)
                        sp.wait_ge(mask_stored, B * 16)
                        sp.wait_ge(q_stored, B * PARTS_STORES)
                        sp.wait_ge(k_stored, B * PARTS_STORES)

                    @block.scalar
                    def _(act):
                        for dst, src in ((coef[:, 0:3], row(rby)), (rden[:], row(freq)), (posc[:], pos),
                                         (gam_row[:], row(gamma)), (beta_row[:], row(beta)), (bo_row[:], row(bo)),
                                         (bv_row[:], row(bv)), (gb_row[:], row(gate_b)), (order[:], row(rank_in)),
                                         (bqk[:, 0:1], bq), (bqk[:, 1:2], bk)):
                            act.dma_start(dst, src).then_inc(vectors_in, 16)
                        act.wait_ge(setup_done, 1)
                        nc.scalar.activation(ROOT, DEN2, ACT.Sqrt).then_inc(root_ready, 1)
                        act.wait_ge(angle_ready, 1)
                        nc.scalar.activation(pe_[:, :, 0:D:2], ang[:], ACT.Sin).then_inc(sine_ready, 1)
                        nc.scalar.activation(half_sin[:], ang[:], ACT.Sin, scale=0.5).then_inc(sine_ready, 1)
                        act.wait_ge(var_ready, 1)
                        nc.scalar.activation(std, var, ACT.Sqrt).then_inc(std_ready, 1)
                        def front(b, first=False):
                            if not first:
                                act.wait_ge(gate_ready, b)
                                act.wait_ge(xn_split, b)
                            act.wait_ge(xn_turned, b + 1)
                            nc.scalar.copy(xnT[:], two_banks(0)).then_inc(xnT_ready, 1)
                            nc.scalar.copy(XTH[:, bass.ds(b * S, S)], two_banks(0)).then_inc(xnT_ready, 1)
                            act.wait_ge(xp_turned, b + 1)
                            nc.scalar.copy(xpT[:], two_banks(2)).then_inc(xpT_ready, 1)
                            act.wait_ge(prob_in, b + 1)
                            nc.scalar.activation(gate[:, 2], gate[:, 1], ACT.Exp).then_inc(prob_exp, 1)
                            act.wait_ge(q_scaled, 1)
                            if not first:
                                act.wait_ge(q_parts, b)
                                act.wait_ge(q_stored, b * PARTS_STORES)
                            act.wait_ge(q_ready, b + 1)
                            nc.scalar.activation(q32[:], two_banks(4), ACT.Identity, bias=bqk[:, 0:1],
                                                 scale=QSCALE).then_inc(q_read, 1)
                            nc.scalar.activation(parts[:, 0, 0, :], two_banks(4), ACT.Identity, bias=bqk[:, 0:1],
                                                 scale=QSCALE).then_inc(q_read, 1)
                            if not first:
                                act.wait_ge(k_parts, b)
                                act.wait_ge(k_stored, b * PARTS_STORES)
                            act.wait_ge(k_ready, b + 1)
                            nc.scalar.activation(k32[:], two_banks(0), ACT.Identity, bias=bqk[:, 1:2]).then_inc(k_read, 1)
                            nc.scalar.activation(parts[:, 1, 0, :], two_banks(0), ACT.Identity,
                                                 bias=bqk[:, 1:2]).then_inc(k_read, 1)
                            act.wait_ge(q_rest, b + 1)
                            nc.scalar.copy(parts[:, 0, 1, :], q32[:]).then_inc(q_second, 1)
                            act.wait_ge(k_rest, b + 1)
                            nc.scalar.copy(parts[:, 1, 1, :], k32[:]).then_inc(k_second, 1)
                            if not first:
                                act.wait_ge(mask_stored, b * 16)
                            act.wait_ge(mask_turned, b + 1)
                            nc.scalar.copy(maskT[:], bank[0:E, 6:8, :].rearrange("p c s -> p (c s)")).then_inc(maskT_ready, 1)
                            if not first:
                                act.wait_ge(low_ready, 2 * b)
                            act.wait_ge(experts_in, b * (3 * 16) + 3 * 16)
                            pair = bass.ds(b * (E // B), E // B)
                            nc.scalar.copy(W1H[:, pair, :], raw[:, 0]).then_inc(high_ready, 1)
                            nc.scalar.copy(W2H[:, pair, :], raw[:, 1]).then_inc(high_ready, 1)

                        front(0, first=True)
                        with act.Fori(1, B) as b:
                            front(b)
                    @block.vector
                    def _(dve):
                        v = nc.vector
                        ch = Chain(dve, dve_chain)
                        dve.wait_ge(vectors_in, 11 * 16)
                        v.tensor_scalar(OUT_FACTOR, YELLOW, EPS_ADAPTIVE, 1.0, ALU.mult, ALU.add)
                        v.tensor_scalar(LN_EPS, BLUE, 0.1, 1.0, ALU.mult, ALU.add)
                        v.tensor_scalar(QSCALE, RED, 0.1, 1.0, ALU.mult, ALU.add)
                        v.tensor_scalar(GAM, RED, 0.1, 1.0, ALU.mult, ALU.add)
                        v.tensor_scalar(TMP, YELLOW, PHASE, 1.0, ALU.mult, ALU.add)
                        ch.link(v.tensor_scalar(DEN2, RED, TENSION, 1.0, ALU.mult, ALU.add))
                        v.tensor_scalar(LN_EPS, LN_EPS, 1e-5, None, ALU.mult)
                        v.scalar_tensor_tensor(QSCALE, BLUE, 0.05, QSCALE, ALU.mult, ALU.add)
                        v.scalar_tensor_tensor(GAM, YELLOW, 0.05, GAM, ALU.mult, ALU.add)
                        v.tensor_scalar(rden[:], rden[:], TMP, None, ALU.mult)
                        ch.link(v.tensor_scalar(DEN2, DEN2, float(DK), None, ALU.mult))
                        v.scalar_tensor_tensor(QSCALE, YELLOW, 0.15, QSCALE, ALU.mult, ALU.add).then_inc(setup_done, 1)
                        v.tensor_scalar(gam_row[:], gam_row[:], GAM, None, ALU.mult)
                        ch.link(v.reciprocal(rden[:], rden[:]))
                        ch.link(v.tensor_tensor(ang[:], posc[:].unsqueeze(2).to_broadcast([P, NT, D // 2]),
                                                rden[:].unsqueeze(1).to_broadcast([P, NT, D // 2]), ALU.mult))
                        ch.link(v.tensor_scalar(turns_[:], ang[:], 0.5 / PI, ROUND, ALU.mult, ALU.add))
                        ch.link(v.tensor_scalar(turns_[:], turns_[:], ROUND, None, ALU.subtract))
                        ch.link(v.scalar_tensor_tensor(ang[:], turns_[:], -TWO_PI_HI, ang[:], ALU.mult, ALU.add))
                        ch.link(v.scalar_tensor_tensor(ang[:], turns_[:], -TWO_PI_LO, ang[:], ALU.mult, ALU.add))
                        v.tensor_scalar(ang[:], ang[:], -PI_DOWN, PI_DOWN, ALU.max, ALU.min).then_inc(angle_ready, 1)
                        dve.wait_ge(root_ready, 1)
                        ch.link(v.reciprocal(TMP, ROOT))
                        ch.link(v.scalar_tensor_tensor(TMP, TMP, DEN2, ROOT, ALU.mult, ALU.add))
                        ch.link(v.tensor_scalar(TMP, TMP, 0.5, None, ALU.mult))
                        ch.link(v.reciprocal(TMP, TMP))
                        ch.link(v.tensor_scalar(QSCALE, QSCALE, TMP, None, ALU.mult))
                        v.tensor_scalar(bqk[:, 0:1], bqk[:, 0:1], QSCALE, None, ALU.mult).then_inc(q_scaled, 1)

                        for b in range(B):
                            dve.wait_ge(x_in[b], 16)
                            for i in range(b * NT, (b + 1) * NT):
                                ch.done(v.bn_stats(bn[:, i, :], X[:, i, :]))
                        ch.settle()
                        for i in range(B * NT):
                            ch.done(v.bn_aggr(mean_var[:, i, :], bn[:, i, :]))
                        ch.settle()
                        v.tensor_scalar(var, mean_var[:, :, 1], 1e-5, None, ALU.add).then_inc(var_ready, 1)
                        dve.wait_ge(sine_ready, 2)
                        ch.link(v.tensor_tensor(half_sin[:], half_sin[:], half_sin[:], ALU.mult))
                        v.tensor_scalar(pe_[:, :, 1:D:2], half_sin[:], -2.0, 1.0, ALU.mult, ALU.add).then_inc(pe_ready, 1)
                        dve.wait_ge(std_ready, 1)
                        ch.link(v.reciprocal(rstd, std))
                        ch.link(v.tensor_tensor(rstd, rstd, var, ALU.mult))
                        ch.link(v.tensor_tensor(rstd, rstd, std, ALU.add))
                        ch.link(v.tensor_scalar(rstd, rstd, 0.5, None, ALU.mult))
                        ch.link(v.reciprocal(rstd, rstd))

                        def normalise(b, first=False):
                            if not first:
                                dve.wait_ge(xn_turned, b)
                                dve.wait_ge(xp_ready, b)
                            at = bass.ds(b * NT, NT)
                            v.tensor_tensor(xc[:], tiles(X, b), mean_var[:, at, 0:1].to_broadcast([P, NT, D]),
                                            ALU.subtract).then_inc(centred, 1)
                            dve.wait_ge(centred, b + 1)
                            v.tensor_tensor(xc[:], xc[:], stat[:, 2, at].unsqueeze(2).to_broadcast([P, NT, D]),
                                            ALU.mult).then_inc(xn_ready, 1)

                        GATE_STEPS = 16

                        def front(b, ahead=True):
                            dve.wait_ge(xnT_ready, 2 * b + 2)
                            v.tensor_tensor(XTL[:, bass.ds(b * S, S)], xnT[:], XTH[:, bass.ds(b * S, S)].bitcast(F32),
                                            ALU.subtract).then_inc(xn_split, 1)
                            dve.wait_ge(gate_ready, b + 1)
                            ch.link(v.tensor_tensor(gate[:, 0], bank[:, 7, 0:NT * E].rearrange("p (t e) -> p t e", e=E),
                                                    gb_row[:].unsqueeze(1).to_broadcast([P, NT, E]), ALU.add))
                            ch.link(v.tensor_reduce(few[:, 0], gate[:, 0], AX_X, ALU.max))
                            v.tensor_tensor(gate[:, 1], gate[:, 0], spread(few[:, 0]), ALU.subtract).then_inc(prob_in, 1)
                            if ahead:
                                normalise(b + 1)
                            dve.wait_ge(prob_exp, b + 1)
                            ch.link(v.tensor_reduce(few[:, 1], gate[:, 2], AX_X, ALU.add))
                            ch.link(v.reciprocal(few[:, 1], few[:, 1]))
                            ch.link(v.tensor_tensor(gate[:, 3], gate[:, 2], spread(few[:, 1]), ALU.mult))
                            ch.link(v.tensor_reduce(few[:, 2], gate[:, 3], AX_X, ALU.max))
                            ch.link(v.tensor_tensor(gate[:, 4], gate[:, 3], spread(few[:, 2]), ALU.is_equal))
                            ch.link(v.tensor_tensor(gate[:, 4], gate[:, 4], ranks, ALU.mult))
                            ch.link(v.tensor_reduce(few[:, 3], gate[:, 4], AX_X, ALU.max))
                            ch.link(v.tensor_tensor(gate[:, 5], ranks, spread(few[:, 3]), ALU.is_equal))
                            ch.link(v.scalar_tensor_tensor(gate[:, 3], gate[:, 5], -2.0, gate[:, 3], ALU.mult, ALU.add))
                            ch.link(v.tensor_reduce(few[:, 4], gate[:, 3], AX_X, ALU.max))
                            ch.link(v.tensor_tensor(gate[:, 4], gate[:, 3], spread(few[:, 4]), ALU.is_equal))
                            ch.link(v.tensor_tensor(gate[:, 4], gate[:, 4], ranks, ALU.mult))
                            ch.link(v.tensor_reduce(few[:, 5], gate[:, 4], AX_X, ALU.max))
                            ch.link(v.tensor_tensor(gate[:, 6], ranks, spread(few[:, 5]), ALU.is_equal))
                            v.tensor_tensor(mask[:], gate[:, 5], gate[:, 6], ALU.add).then_inc(mask_ready, 1)
                            dve.wait_ge(v_ready, b + 1)
                            v.tensor_tensor(tiles(V, b), two_banks(2).rearrange("p (t d) -> p t d", d=D),
                                            bv_row[:].unsqueeze(1).to_broadcast([P, NT, D]), ALU.add).then_inc(v_read, 1)
                            dve.wait_ge(q_read, 2 * b + 2)
                            v.tensor_tensor(q32[:], q32[:], parts[:, 0, 0, :], ALU.subtract).then_inc(q_rest, 1)
                            dve.wait_ge(q_second, b + 1)
                            v.tensor_tensor(parts[:, 0, 2, :], q32[:], parts[:, 0, 1, :],
                                            ALU.subtract).then_inc(q_parts, 1)

                        normalise(0, first=True)
                        with dve.Fori(0, B - 1) as b:
                            ch.turn(b, GATE_STEPS)
                            front(b)
                            ch.end_turns(B - 1)
                        front(B - 1, ahead=False)

                    @block.gpsimd
                    def _(pool):
                        tt = nc.gpsimd.tensor_tensor

                        def encode(b, first=False):
                            pool.wait_ge(xn_ready, b + 1)
                            if not first:
                                pool.wait_ge(xp_turned, b)
                                pool.wait_ge(xp_stored, b * 16)
                            tt(xs[:], xc[:], pe_[:], ALU.add).then_inc(xp_ready, 1)

                        def front(b, ahead=True):
                            pool.wait_ge(k_read, 2 * b + 2)
                            tt(k32[:], k32[:], parts[:, 1, 0, :], ALU.subtract).then_inc(k_rest, 1)
                            if ahead:
                                encode(b + 1)
                            pool.wait_ge(k_second, b + 1)
                            tt(parts[:, 1, 2, :], k32[:], parts[:, 1, 1, :], ALU.subtract).then_inc(k_parts, 1)
                            pool.wait_ge(high_ready, 2 * b + 2)
                            pair = bass.ds(b * (E // B), E // B)
                            tt(W1L[:, pair, :], raw[:, 0], W1H[:, pair, :].bitcast(F32),
                               ALU.subtract).then_inc(low_ready, 1)
                            tt(W2L[:, pair, :], raw[:, 1], W2H[:, pair, :].bitcast(F32),
                               ALU.subtract).then_inc(low_ready, 1)

                        pool.wait_ge(pe_ready, 1)
                        encode(0, first=True)
                        with pool.Fori(0, B - 1) as b:
                            front(b)
                        front(B - 1, ahead=False)

                    @block.tensor
                    def _(pe):
                        mm, turned = nc.tensor.matmul, nc.tensor.transpose
                        pe.wait_ge(weights_in, 5 * 16)
                        def front(b, first=False):
                            if not first:
                                pe.wait_ge(k_read, 2 * b)
                            pe.wait_ge(xn_ready, b + 1)
                            for t in range(NT):
                                last = turned(bank[:, t // 4, (t % 4) * P:(t % 4 + 1) * P], xc[:, t, :], ident[:])
                            last.then_inc(xn_turned, 1)
                            if not first:
                                pe.wait_ge(v_read, b)
                            pe.wait_ge(xp_ready, b + 1)
                            for t in range(NT):
                                last = turned(bank[:, 2 + t // 4, (t % 4) * P:(t % 4 + 1) * P], xs[:, t, :], ident[:])
                            last.then_inc(xp_turned, 1)
                            if not first:
                                pe.wait_ge(maskT_ready, b)
                            pe.wait_ge(xnT_ready, 2 * b + 2)
                            for t in range(NT):
                                last = mm(bank[:, 7, t * E:(t + 1) * E], xnT[:, t * P:(t + 1) * P], gw[:], start=True, stop=True)
                            last.then_inc(gate_ready, 1)
                            pe.wait_ge(xpT_ready, b + 1)
                            for c in range(NC):
                                last = mm(bank[:, 4 + c, :], wq[:], xpT[:, c * CH:(c + 1) * CH], start=True, stop=True)
                            last.then_inc(q_ready, 1)
                            for c in range(NC):
                                last = mm(bank[:, c, :], wk[:], xpT[:, c * CH:(c + 1) * CH], start=True, stop=True)
                            last.then_inc(k_ready, 1)
                            for t in range(NT):
                                last = mm(bank[:, 2 + t // 4, (t % 4) * P:(t % 4 + 1) * P], xpT[:, t * P:(t + 1) * P], wv[:],
                                          start=True, stop=True)
                            last.then_inc(v_ready, 1)
                            pe.wait_ge(mask_ready, b + 1)
                            for t in range(NT):
                                last = turned(bank[0:E, 6 + t // 4, (t % 4) * P:(t % 4 + 1) * P], mask[:, t, :], ident[:])
                            last.then_inc(mask_turned, 1)

                        front(0, first=True)
                        with pe.Fori(1, B) as b:
                            front(b)
            HIDDEN = (0, 1, 6, 7)
            CREDIT_SPLIT, CREDIT_USED, CREDIT_RELU, CREDIT_SUM, CREDIT_BASE = 2, 4, 8, 2, 1
            with ExitStack() as one:
                mask_all = sb(one, "mask_all", [P, 2, E, CH], BF16)
                hid = sb(one, "hid", [P, 2, CH])
                HH = sb(one, "HH", [P, FT, CH], F32R)
                HL = sb(one, "HL", [P, FT, CH], F32R)
                masked = sb(one, "masked", [P, 2, CH])
                acc = sb(one, "acc", [P, CH])

                with nc.Block() as block:
                    @block.sync
                    def _(sp):
                        def load_mask(c):
                            b, half = c >> 1, c & 1
                            if not isinstance(c, int):
                                b = b & (B - 1)
                                sp.compute_val(b)
                                sp.compute_val(half)
                                sp.wait_ge(mask_spread, c * 16)
                                sp.wait_ge(sum_read, (c - 1) * E + CREDIT_SUM)
                            elif c:
                                sp.wait_ge(mask_spread, c * 16)
                            sp.dma_start(mask_all[:, bass.ds(half, 1)].rearrange("p o e s -> p (o e) s"),
                                         mask_rows[bass.ds(b, 1), :, bass.ds(half * CH, CH)].rearrange(
                                             "o e s -> (o e) s").partition_broadcast(P)).then_inc(mask_spread, 16)

                        load_mask(0)
                        load_mask(1)
                        with sp.Fori(2, CHUNKS) as c:
                            load_mask(c)
                        sp.wait_ge(mask_spread, CHUNKS * 16)

                    @block.scalar
                    def _(act):
                        with act.Fori(0, CHUNKS) as c:
                            for j in range(TILES):
                                e, t, n = j // FT, j % FT, c * TILES + j
                                act.wait_ge(hid_ready, n + 1)
                                act.wait_ge(hid_split, n - 1 + CREDIT_SPLIT)
                                act.wait_ge(hid_used, n - 3 + CREDIT_USED)
                                nc.scalar.activation(hid[:, j % 2, :], bank[:, HIDDEN[t], :], ACT.Relu,
                                                     bias=B1[:, e, t:t + 1]).then_inc(hid_relu, 1)
                                nc.scalar.activation(HH[:, t, :], bank[:, HIDDEN[t], :], ACT.Relu,
                                                     bias=B1[:, e, t:t + 1]).then_inc(hid_relu, 1)

                    @block.vector
                    def _(dve):
                        v = nc.vector
                        v.memset(masked[:, 0, 0:1], 0.0).then_inc(hid_split, CREDIT_SPLIT)
                        v.memset(masked[:, 0, 1:2], 0.0).then_inc(hid_used, CREDIT_USED)
                        v.memset(masked[:, 0, 2:3], 0.0).then_inc(hid_relu, CREDIT_RELU)
                        v.memset(masked[:, 0, 3:4], 0.0).then_inc(sum_read, CREDIT_SUM)
                        v.memset(masked[:, 0, 4:5], 0.0).then_inc(base_ready, CREDIT_BASE)

                        def split(c, j):
                            n = c * TILES + j
                            dve.wait_ge(hid_relu, 2 * n + 2 + CREDIT_RELU)
                            v.tensor_tensor(HL[:, j % FT, :], hid[:, j % 2, :], HH[:, j % FT, :].bitcast(F32),
                                            ALU.subtract).then_inc(hid_split, 1)

                        def take(c, e, first=False):
                            n = c * E + e
                            dve.wait_ge(hid_used, n * FT + FT + CREDIT_USED)
                            if e == 0:
                                dve.wait_ge(mask_spread, c * 16 + 16)
                                if not first:
                                    dve.wait_ge(acc_turned, c)
                            dst = acc[:] if e == 0 else masked[:, e % 2, :]
                            v.scalar_tensor_tensor(dst, bank[:, 2 + e % 2, :], B2[:, e:e + 1],
                                                   mask_all[:, bass.ds(c & 1, 1), e, :].rearrange("p o s -> p (o s)"),
                                                   ALU.add, ALU.mult).then_inc(sum_read, 1)

                        def add(c, e):
                            dve.wait_ge(sum_read, c * E + e + 1 + CREDIT_SUM)
                            if e > 1:
                                dve.wait_ge(acc_ready, c * (E - 1) + e - 1)
                            v.tensor_tensor(acc[:], acc[:], masked[:, e % 2, :], ALU.add).then_inc(acc_ready, 1)

                        def give(c):
                            dve.wait_ge(acc_turned, c + 1)
                            xt = X[:, bass.ds(c * (NT // NC), NT // NC), :]
                            v.tensor_tensor(xt, xt, bank[:, 5, :].rearrange("p (t d) -> p t d", d=D),
                                            ALU.add).then_inc(base_ready, 1)

                        def chunk(c, first=False):
                            for j in range(TILES):
                                e = j // FT
                                split(c, j)
                                if j % FT == 2 and e:
                                    take(c, e - 1, first)
                                if j % FT == 3 and e > 1:
                                    add(c, e - 1)
                                if not first and j == 2:
                                    take(c - 1, E - 1)
                                if not first and j == 3:
                                    add(c - 1, E - 1)
                                if not first and j == 7:
                                    give(c - 1)

                        dve.wait_ge(beta_added, B)
                        chunk(0, first=True)
                        with dve.Fori(1, CHUNKS) as c:
                            chunk(c)
                        take(CHUNKS - 1, E - 1)
                        add(CHUNKS - 1, E - 1)
                        give(CHUNKS - 1)

                    @block.gpsimd
                    def _(pool):
                        for b in range(B):
                            xt = X[:, b * NT:(b + 1) * NT, :]
                            nc.gpsimd.tensor_tensor(xt, xt, beta_row[:].unsqueeze(1).to_broadcast([P, NT, D]),
                                                    ALU.add).then_inc(beta_added, 1)

                    @block.tensor
                    def _(pe):
                        mm, turned = nc.tensor.matmul, nc.tensor.transpose

                        def first_weights(c, j):
                            e, t, n = j // FT, j % FT, c * TILES + j
                            pe.wait_ge(hid_relu, 2 * (n - 3) + CREDIT_RELU)
                            dst, cols, at = bank[:, HIDDEN[t], :], slice(t * P, (t + 1) * P), bass.ds(c * CH, CH)
                            mm(dst, W1H[:, e, cols], XTH[:, at], start=True, stop=False)
                            mm(dst, W1H[:, e, cols], XTL[:, at], start=False, stop=False)
                            mm(dst, W1L[:, e, cols], XTH[:, at], start=False, stop=True).then_inc(hid_ready, 1)

                        def second_weights(c, j):
                            e, t = j // FT, j % FT
                            if t == 0:
                                pe.wait_ge(sum_read, c * E + e - 1 + CREDIT_SUM)
                            pe.wait_ge(hid_split, c * TILES + j + 1 + CREDIT_SPLIT)
                            dst, cols = bank[:, 2 + e % 2, :], slice(t * P, (t + 1) * P)
                            mm(dst, W2H[:, e, cols], HH[:, t, :], start=(t == 0), stop=False)
                            mm(dst, W2H[:, e, cols], HL[:, t, :], start=False, stop=False)
                            last = mm(dst, W2L[:, e, cols], HH[:, t, :], start=False, stop=(t == FT - 1))
                            last.then_inc(hid_used, 1)

                        def turn(c):
                            pe.wait_ge(acc_ready, c * (E - 1) + E - 1)
                            pe.wait_ge(base_ready, c + CREDIT_BASE)
                            for t in range(NT // NC):
                                last = turned(bank[:, 5, t * P:(t + 1) * P], acc[:, t * P:(t + 1) * P], ident[:])
                            last.then_inc(acc_turned, 1)

                        def chunk(c, first=False):
                            for j in range(TILES):
                                first_weights(c, j)
                                if j >= LAG:
                                    second_weights(c, j - LAG)
                                elif not first:
                                    second_weights(c - 1, TILES + j - LAG)
                                if j == 5 and not first:
                                    turn(c - 1)

                        chunk(0, first=True)
                        with pe.Fori(1, CHUNKS) as c:
                            chunk(c)
                        second_weights(CHUNKS - 1, TILES - 2)
                        second_weights(CHUNKS - 1, TILES - 1)
                        turn(CHUNKS - 1)

        STEPS = NT
        CREDIT_AV, CREDIT_EXP, CREDIT_ITEM, CREDIT_PAIR = STEPS, 2, 2, 1
        CREDIT_MAX, CREDIT_SUMS = PARTS * 16, 2 * U * 16
        UC = U * S
        LOADS = 2 * PARTS
        CREDIT_UNIT = LOADS * 16
        with ExitStack() as two:
            QS = sb(two, "QS", [KR2, RING * UC], BF16)
            KS = sb(two, "KS", [KR2, RING * UC], BF16)
            probs = sb(two, "probs", [P, 2, U, CH])
            VS = sb(two, "VS", [P, STEPS, U, 32])
            row_max = sb(two, "row_max", [P, ITEMS])
            neg_max = sb(two, "neg_max", [P, ITEMS])
            maxT = sb(two, "maxT", [ITEMS, P])
            zeros = sb(two, "zeros", [ITEMS, P])
            max_rest = sb(two, "max_rest", [ITEMS, P])
            max_parts = sb(two, "max_parts", [ITEMS, PARTS, P], BF16)
            sums = sb(two, "sums", [P, 2, CH])
            blank = sb(two, "blank", [KR - PROD, S], BF16)
            one_row = sb(two, "one_row", [PARTS, S], BF16)

            with nc.Block() as block:
                @block.sync
                def _(sp):
                    def ahead(*values):
                        for value in values:
                            if not isinstance(value, int):
                                sp.compute_val(value)

                    def load_unit(u):
                        slot = u & (RING - 1)
                        ahead(slot)
                        cols = bass.ds(slot * UC, UC)
                        sp.wait_ge(unit_in, u * (LOADS * 16) + CREDIT_UNIT)
                        for i in range(PARTS):
                            rows = slice(i * PARTS * DK, (i + 1) * PARTS * DK)
                            sp.dma_start(KS[rows, cols], qk_parts[1, bass.ds(u, 1)].rearrange(
                                "o n d u s -> (o n d) (u s)")).then_inc(unit_in, 16)
                            q = qk_parts[0, bass.ds(u, 1), i].rearrange("o d u s -> (o d) (u s)")
                            sp.dma_start(QS[rows, cols], q.unsqueeze(0).to_broadcast([PARTS, DK, UC])).then_inc(unit_in, 16)

                    def load_max(v):
                        slot = v & (2 * RING - 1)
                        ahead(slot)
                        sp.wait_ge(maxT_parts, v + 2)
                        sp.wait_ge(max_in, v * (PARTS * 16) + CREDIT_MAX)
                        for n in range(PARTS):
                            sp.dma_start(QS[KR + n:KR + n + 1, bass.ds(slot * HALF, HALF)],
                                         max_parts[:, n, :]).then_inc(max_in, 16)

                    def store_sums(w):
                        b, g, c = (w >> 3) & (B - 1), (w >> 1) & (NG - 1), w & (NC - 1)
                        ahead(b, g, c)
                        sp.wait_ge(sums_out, w + 1 + CREDIT_PAIR)
                        sp.wait_ge(sums_stored, w * (U * 16) + CREDIT_SUMS)
                        for u in range(U):
                            dst = attn_sums[:, bass.ds(b, 1), bass.ds(g * (U * DK) + u * DK, DK), bass.ds(c * CH, CH)]
                            sp.dma_start(dst.rearrange("m o d q -> (m o) d q"),
                                         sums[32 * u:32 * u + 2 * DK, bass.ds(c, 1), :]).then_inc(sums_stored, 16)

                    with sp.Fori(0, RING) as u:
                        load_unit(u)
                    with sp.Fori(0, LEAD) as v:
                        load_max(v)
                    load_max(LEAD)
                    with sp.Fori(0, NU - RING) as u:
                        store_sums(2 * u)
                        load_max(2 * u + (LEAD + 1))
                        store_sums(2 * u + 1)
                        ahead((u + RING) & (RING - 1))
                        sp.wait_ge(av_done, u * (NC * STEPS) + (NC * STEPS + CREDIT_AV))
                        load_unit(u + RING)
                        load_max(2 * u + (LEAD + 2))
                    with sp.Fori(2 * (NU - RING), NW - LEAD - 1) as w:
                        store_sums(w)
                        load_max(w + (LEAD + 1))
                    with sp.Fori(NW - LEAD - 1, NW) as w:
                        store_sums(w)
                    sp.wait_ge(sums_stored, NW * (U * 16) + CREDIT_SUMS)

                @block.tensor
                def _(pe):
                    mm = nc.tensor.matmul

                    def max_item(i, v):
                        if i == 0:
                            pe.wait_ge(unit_in, (v >> 1) * (LOADS * 16) + (LOADS * 16 + CREDIT_UNIT))
                        pe.wait_ge(item_read, v * ITEMS + (i - 1 + CREDIT_ITEM))
                        head, tile = i // NT, i % NT
                        at = (v & 7) * HALF + head * S
                        for c in range(NC):
                            last = mm(bank[:, 2 * (i % 2) + c, :], QS[0:KR, bass.ds(at + tile * P, P)],
                                      KS[0:KR, bass.ds(at + c * CH, CH)], start=True, stop=True)
                        last.then_inc(item_ready, 1)

                    def turn_max(v):
                        pe.wait_ge(max_ready, v + 1)
                        nc.tensor.transpose(bank[0:ITEMS, 7, 0:P], neg_max[:], ident[:]).then_inc(max_turned, 1)

                    def logits(w, t, u):
                        if t == 0 and u == 0:
                            pe.wait_ge(max_in, (w >> 1) * (2 * PARTS * 16) + (2 * PARTS * 16 + CREDIT_MAX))
                        pe.wait_ge(exp_out, w * (STEPS * U) + (t * U + u - 1 + CREDIT_EXP))
                        at = ((w >> 1) & (RING - 1)) * UC + u * S
                        mm(bank[:, 4 + u % 2, :], KS[:, bass.ds(at + t * P, P)],
                           QS[:, bass.ds(at + (w & 1) * CH, CH)], start=True, stop=True).then_inc(logits_ready, 1)

                    def product(w, t):
                        if t == 0:
                            pe.wait_ge(sums_out, w + CREDIT_PAIR)
                        pe.wait_ge(v_staged, (w >> 1) * STEPS + (t + 1))
                        pe.wait_ge(exp_out, w * (STEPS * U) + (t * U + U + CREDIT_EXP))
                        for u in range(U):
                            last = mm(bank[32 * u:32 * u + 32, 6, :], VS[:, t, u, :], probs[:, t % 2, u, :],
                                      start=(t == 0), stop=(t == STEPS - 1))
                        last.then_inc(av_done, 1)

                    def pair(w, items=True, turn=True, before=True):
                        for t in range(STEPS):
                            logits(w, t, 0)
                            logits(w, t, 1)
                            if t:
                                product(w, t - 1)
                            elif before:
                                product(w - 1, STEPS - 1)
                            logits(w, t, 2)
                            logits(w, t, 3)
                            if turn and t == 1:
                                turn_max(w + (LEAD - 1))
                            if items:
                                max_item(2 * t, w + LEAD)
                                max_item(2 * t + 1, w + LEAD)

                    pe.wait_ge(pads_first, 2 * 16)
                    for i in range(ITEMS):
                        max_item(i, 0)
                    pe.wait_ge(pads_rest, 3 * 16)
                    with pe.Fori(1, LEAD) as v:
                        for i in range(ITEMS):
                            max_item(i, v)
                            if i == 3:
                                turn_max(v - 1)
                    pair(0, before=False)
                    with pe.Fori(1, NW - LEAD) as w:
                        pair(w)
                    pair(NW - LEAD, items=False)
                    with pe.Fori(NW - LEAD + 1, NW) as w:
                        pair(w, items=False, turn=False)
                    product(NW - 1, STEPS - 1)

                @block.scalar
                def _(act):
                    def pad(dst, src, signal):
                        rows, times = src.shape[0], dst.shape[1] // S
                        act.dma_start(dst.rearrange("p (n s) -> p n s", s=S),
                                      src[:].unsqueeze(1).to_broadcast([rows, times, S])).then_inc(signal, 16)

                    act.wait_ge(blank_ready, 2)
                    for operand in (KS, QS):
                        pad(operand[PROD:KR, 0:UC], blank, pads_first)
                    for operand in (KS, QS):
                        pad(operand[PROD:KR, UC:RING * UC], blank, pads_rest)
                    pad(KS[KR:KR2, :], one_row, pads_rest)
                    with act.Fori(0, NW) as w:
                        for t in range(STEPS):
                            act.wait_ge(av_done, w * STEPS + (t - 1 + CREDIT_AV))
                            for u in range(U):
                                act.wait_ge(logits_ready, w * (STEPS * U) + (t * U + u + 1))
                                nc.scalar.activation(probs[:, t % 2, u, :], bank[:, 4 + u % 2, :],
                                                     ACT.Exp).then_inc(exp_out, 1)

                @block.vector
                def _(dve):
                    v_ = nc.vector
                    v_.memset(blank[:], 0.0).then_inc(blank_ready, 1)
                    v_.memset(one_row[:], 1.0).then_inc(blank_ready, 1)
                    v_.memset(row_max[:, 0:1], 0.0).then_inc(item_read, CREDIT_ITEM)
                    v_.memset(row_max[:, 1:2], 0.0).then_inc(exp_out, CREDIT_EXP)
                    v_.memset(row_max[:, 2:3], 0.0).then_inc(av_done, CREDIT_AV)
                    v_.memset(row_max[:, 3:4], 0.0).then_inc(sums_stored, CREDIT_SUMS)
                    v_.memset(row_max[:, 4:5], 0.0).then_inc(max_in, CREDIT_MAX)
                    v_.memset(row_max[:, 7:8], 0.0).then_inc(unit_in, CREDIT_UNIT)
                    v_.memset(row_max[:, 5:6], 0.0).then_inc(sums_out, CREDIT_PAIR)
                    v_.memset(row_max[:, 6:7], 0.0).then_inc(maxT_parts, 1)

                    def reduce_item(i, v):
                        dve.wait_ge(item_ready, v * ITEMS + (i + 1))
                        v_.tensor_reduce(row_max[:, i:i + 1], two_banks(2 * (i % 2)), AX_X,
                                         ALU.max).then_inc(item_read, 1)

                    def negate(v):
                        dve.wait_ge(item_read, v * ITEMS + (ITEMS + CREDIT_ITEM))
                        v_.tensor_scalar(neg_max[:], row_max[:], -1.0, None, ALU.mult).then_inc(max_ready, 1)
                        dve.wait_ge(max_ready, v + 1)

                    def take_turned(v):
                        dve.wait_ge(max_turned, v + 1)
                        dve.wait_ge(maxT_parts, v + 1)
                        v_.tensor_copy(maxT[:], bank[0:ITEMS, 7, 0:P]).then_inc(maxT_ready, 1)

                    def take_sums(w):
                        dve.wait_ge(av_done, w * STEPS + (STEPS + CREDIT_AV))
                        dve.wait_ge(sums_stored, w * (U * 16) + CREDIT_SUMS - U * 16)
                        v_.tensor_copy(sums[:, bass.ds(w & 1, 1), :].rearrange("p o q -> p (o q)"),
                                       bank[:, 6, :]).then_inc(sums_out, 1)

                    def pair(w, items=True, turn=True, before=True):
                        if before:
                            take_sums(w - 1)
                        for t in range(STEPS):
                            if items:
                                reduce_item(2 * t, w + LEAD)
                            if turn and t == 2:
                                take_turned(w + (LEAD - 1))
                            if items:
                                reduce_item(2 * t + 1, w + LEAD)
                        if items:
                            negate(w + LEAD)

                    for i in range(ITEMS):
                        reduce_item(i, 0)
                    negate(0)
                    with dve.Fori(1, LEAD) as v:
                        for i in range(ITEMS):
                            reduce_item(i, v)
                            if i == 4:
                                take_turned(v - 1)
                        negate(v)
                    pair(0, before=False)
                    with dve.Fori(1, NW - LEAD) as w:
                        pair(w)
                    pair(NW - LEAD, items=False)
                    with dve.Fori(NW - LEAD, NW) as w:
                        take_sums(w)

                @block.gpsimd
                def _(pool):
                    ch = Chain(pool, pool_chain)

                    def stage_v(u, t):
                        pool.wait_ge(av_done, u * (NC * STEPS) + (t + 1))
                        pool.wait_ge(ones_set, 1)
                        at = bass.ds(((u >> 2) & (B - 1)) * NT + t, 1)
                        nc.gpsimd.tensor_copy(VS[:, t, :, 0:DK],
                                              V[:, at, bass.ds((u & (NG - 1)) * (U * DK), U * DK)].rearrange(
                                                  "p o (u d) -> p (o u) d", d=DK)).then_inc(v_staged, 1)

                    def split_max(v):
                        pool.wait_ge(maxT_ready, v + 1)
                        pool.wait_ge(max_in, v * (PARTS * 16) + CREDIT_MAX)
                        pool.wait_ge(ones_set, 1)
                        ch.link(nc.gpsimd.tensor_tensor(max_parts[:, 0, :], maxT[:], zeros[:], ALU.add))
                        ch.link(nc.gpsimd.tensor_tensor(max_rest[:], maxT[:], max_parts[:, 0, :], ALU.subtract))
                        ch.link(nc.gpsimd.tensor_tensor(max_parts[:, 1, :], max_rest[:], zeros[:], ALU.add))
                        nc.gpsimd.tensor_tensor(max_parts[:, 2, :], max_rest[:], max_parts[:, 1, :],
                                                ALU.subtract).then_inc(maxT_parts, 1)

                    nc.gpsimd.memset(zeros[:], 0.0)
                    nc.gpsimd.memset(VS[:], 1.0).then_inc(ones_set, 1)
                    for t in range(STEPS):
                        stage_v(0, t)
                    split_max(0)
                    split_max(1)
                    with pool.Fori(0, NU - 1) as u:
                        ch.turn(u, 2 * 3)
                        split_max(2 * u + 2)
                        stage_v(u + 1, 0)
                        stage_v(u + 1, 1)
                        split_max(2 * u + 3)
                        for t in range(2, STEPS):
                            stage_v(u + 1, t)
                        ch.end_turns(NU - 1)

        with ExitStack() as three:
            numer = sb(three, "numer", [P, B, S])
            denom = sb(three, "denom", [P, B, S])
            XP = sb(three, "XP", [P, B * NT, D])
            outT = sb(three, "outT", [P, 2, S])
            y = sb(three, "y", [P, 2, NT, D])
            result = sb(three, "result", [P, 2, NT, D])
            bn2 = sb(three, "bn2", [P, NT, 6])
            mean_var2 = sb(three, "mean_var2", [P, NT, 2])
            v8, s8, r8, shift = (sb(three, n, [P, 2, NT]) for n in ("v8", "s8", "r8", "shift"))

            with nc.Block() as block:
                @block.sync
                def _(sp):
                    ov = out.rearrange("b (t p) d -> b p t d", p=P)
                    for b in range(B):
                        for m, dst in ((1, denom), (0, numer)):
                            sp.dma_start(dst[:, b, :], attn_sums[m, b]).then_inc(tail_in[b], 16)
                        sp.dma_start(XP[:, b * NT:(b + 1) * NT, :],
                                     xp_rows[b].rearrange("(t p) d -> p t d", p=P)).then_inc(tail_xp[b], 16)
                    for b in range(B):
                        sp.wait_ge(result_ready, b + 1)
                        sp.dma_start(ov[b], result[:, b % 2]).then_inc(result_out, 16)
                        sp.wait_ge(result_out, b * 16 + 16)

                @block.scalar
                def _(act):
                    for b in range(B):
                        act.wait_ge(row_var, b + 1)
                        nc.scalar.activation(s8[:, b % 2], v8[:, b % 2], ACT.Sqrt).then_inc(row_std, 1)
                        act.wait_ge(row_scale, b + 1)
                        for t in range(NT):
                            last = nc.scalar.activation(y[:, b % 2, t, :], y[:, b % 2, t, :], ACT.Identity,
                                                        bias=shift[:, b % 2, t:t + 1], scale=r8[:, b % 2, t:t + 1])
                        last.then_inc(row_norm, NT)

                @block.tensor
                def _(pe):
                    for b in range(B):
                        pe.wait_ge(outT_ready, b + 1)
                        if b >= 2:
                            pe.wait_ge(y_ready, b - 1)
                        for t in range(NT):
                            last = nc.tensor.matmul(bank[:, 2 * (b % 2) + t // 4, (t % 4) * P:(t % 4 + 1) * P],
                                                    outT[:, b % 2, t * P:(t + 1) * P], wo[:], start=True, stop=True)
                        last.then_inc(proj_ready, 1)

                @block.vector
                def _(dve):
                    v = nc.vector
                    ch = Chain(dve, tail_chain)

                    def divide(b):
                        dve.wait_ge(tail_in[b], 32)
                        if b >= 2:
                            dve.wait_ge(proj_ready, b - 1)
                        ch.link(v.reciprocal(denom[:, b, :], denom[:, b, :]))
                        v.scalar_tensor_tensor(outT[:, b % 2, :], numer[:, b, :], OUT_FACTOR, denom[:, b, :],
                                               ALU.mult, ALU.mult).then_inc(outT_ready, 1)

                    def statistics(b):
                        dve.wait_ge(proj_ready, b + 1)
                        dve.wait_ge(xpb_ready, b + 1)
                        if b >= 2:
                            dve.wait_ge(result_ready, b - 1)
                        h = b % 2
                        v.tensor_tensor(y[:, h], two_banks(2 * h).rearrange("p (t d) -> p t d", d=D),
                                        XP[:, b * NT:(b + 1) * NT, :], ALU.add).then_inc(y_ready, 1)
                        dve.wait_ge(y_ready, b + 1)
                        for t in range(NT):
                            ch.done(v.bn_stats(bn2[:, t, :], y[:, h, t, :]))
                        ch.settle()
                        for t in range(NT):
                            ch.done(v.bn_aggr(mean_var2[:, t, :], bn2[:, t, :]))
                        ch.settle()
                        v.tensor_scalar(v8[:, h], mean_var2[:, :, 1], LN_EPS, None, ALU.add).then_inc(row_var, 1)

                    def scale_rows(b):
                        h = b % 2
                        dve.wait_ge(row_std, b + 1)
                        ch.link(v.reciprocal(r8[:, h], s8[:, h]))
                        ch.link(v.tensor_tensor(r8[:, h], r8[:, h], v8[:, h], ALU.mult))
                        ch.link(v.tensor_tensor(r8[:, h], r8[:, h], s8[:, h], ALU.add))
                        ch.link(v.tensor_scalar(r8[:, h], r8[:, h], 0.5, None, ALU.mult))
                        ch.link(v.reciprocal(r8[:, h], r8[:, h]))
                        v.scalar_tensor_tensor(shift[:, h], mean_var2[:, :, 0], -1.0, r8[:, h], ALU.mult,
                                               ALU.mult).then_inc(row_scale, 1)
                        dve.wait_ge(row_scale, b + 1)

                    def gammas(b):
                        h = b % 2
                        dve.wait_ge(row_norm, (b + 1) * NT)
                        v.tensor_tensor(y[:, h], y[:, h], gam_row[:].unsqueeze(1).to_broadcast([P, NT, D]),
                                        ALU.mult).then_inc(gam_done, 1)

                    divide(0)
                    for b in range(B):
                        statistics(b)
                        if b + 1 < B:
                            divide(b + 1)
                        scale_rows(b)
                        if b:
                            gammas(b - 1)
                    gammas(B - 1)

                @block.gpsimd
                def _(pool):
                    tt = nc.gpsimd.tensor_tensor

                    def residual(b):
                        pool.wait_ge(tail_xp[b], 16)
                        xp = XP[:, b * NT:(b + 1) * NT, :]
                        tt(xp, xp, bo_row[:].unsqueeze(1).to_broadcast([P, NT, D]), ALU.add).then_inc(xpb_ready, 1)

                    residual(0)
                    residual(1)
                    for b in range(B):
                        if b + 2 < B:
                            residual(b + 2)
                        if b >= 2:
                            pool.wait_ge(result_out, (b - 1) * 16)
                        pool.wait_ge(gam_done, b + 1)
                        tt(result[:, b % 2], y[:, b % 2], X[:, b * NT:(b + 1) * NT, :], ALU.add).then_inc(result_ready, 1)


def kernel(**inputs):
    import numpy as np
    import concourse.bacc as bacc
    from concourse.bass_utils import run_bass_kernel_spmd as run

    def take(name):
        return np.asarray(inputs[name])

    nc = bacc.Bacc("TRN2", target_bir_lowering=False, num_devices=1)
    laid = {
        "x": take("L0_attn_x"), "rby": take("L0_attn_rby"),
        "wqT": take("L0_attn_Wq").T, "bq": take("L0_attn_bq").reshape(P, 1),
        "wkT": take("L0_attn_Wk").T, "bk": take("L0_attn_bk").reshape(P, 1),
        "wvT": take("L0_attn_Wv").T, "bv": take("L0_attn_bv"),
        "woT": take("L0_attn_Wo").T, "bo": take("L0_attn_bo"),
        "gamma": take("L0_attn_ln_gamma"), "beta": take("L0_attn_ln_beta"),
        "gate_w": take("L0_ffn_gate_w"), "gate_b": take("L0_ffn_gate_b"),
        "w1": take("L0_ffn_w1"), "b1T": take("L0_ffn_b1").reshape(E, FT, P).transpose(2, 0, 1),
        "w2": take("L0_ffn_w2"), "b2T": take("L0_ffn_b2").T,
        "ident_in": np.eye(P, dtype=np.float32),
        "freq": np.power(np.float32(10000.0), 2.0 * np.arange(0, D, 2, dtype=np.float32) / np.float32(D)).astype(np.float32),
        "pos": (np.arange(P, dtype=np.float32)[:, None] + np.float32(P) * np.arange(NT, dtype=np.float32)[None, :]),
        "rank_in": np.arange(E, 0, -1).astype(np.float32),
    }
    arrays, args = {}, []
    for name, a in laid.items():
        arrays[f"in_{name}"] = np.ascontiguousarray(a)
        args.append(nc.dram_tensor(f"in_{name}", arrays[f"in_{name}"].shape, mybir.dt.from_np(a.dtype),
                                   kind="ExternalInput").ap())
    out = nc.dram_tensor("out_0", (B, S, D), F32, kind="ExternalOutput").ap()
    build(nc, *args, out)
    return run(nc, [arrays], core_ids=[0]).results[0]["out_0"]
```

```python
from contextlib import ExitStack

import concourse.bass as bass
from concourse import mybir

F32 = mybir.dt.float32
BF16 = mybir.dt.bfloat16
F32R = mybir.dt.float32r
ALU = mybir.AluOpType
ACT = mybir.ActivationFunctionType
AX_X = mybir.AxisListType.X

P = 128
B, S, D = 4, 1024, 128
H, DK = 16, 8
NT = S // P
E, F = 8, 512
FT = F // P
CH = 512
NC = S // CH
U = 4
NG = H // U
NU = B * NG
NW = NU * NC
PARTS = 3
PROD = PARTS * PARTS * DK
KR = 96
KR2 = KR + PARTS
RING = 4
HALF = U * CH
ITEMS = U * NT // NC
LEAD = 2
PI = 3.14159265358979
PI_DOWN = 3.1415925
TILES = E * FT
CHUNKS = B * NC
LAG = 2
PARTS_STORES = PARTS * 16
TENSION = abs(1.0 - 1.0)
PHASE = 0.1
EPS_ADAPTIVE = 0.1 * 1.2246467991473532e-16
ROUND = 1.5 * 2.0 ** 23
TWO_PI_HI = 6.28125
TWO_PI_LO = 6.283185307179586 - 6.28125


class Chain:

    def __init__(self, eng, sem):
        self.eng, self.sem, self.n, self.base, self.outer = eng, sem, 0, 0, []

    def done(self, ins):
        ins.then_inc(self.sem, 1)
        self.n += 1

    def settle(self):
        self.eng.wait_ge(self.sem, self.base + self.n)

    def link(self, ins):
        self.done(ins)
        self.settle()

    def turn(self, i, per_turn):
        self.outer.append((self.base, self.n, per_turn))
        self.base = self.base + i * per_turn

    def end_turns(self, turns):
        self.base, start, per_turn = self.outer.pop()
        assert self.n - start == per_turn, (self.n - start, per_turn)
        self.n = start + turns * per_turn


def row(vec, n=P):
    return vec.partition_broadcast(n)


def build(nc, x, rby, wqT, bq, wkT, bk, wvT, bv, woT, bo, gamma, beta, gate_w, gate_b, w1, b1T, w2, b2T,
          ident_in, freq, pos, rank_in, out):
    with ExitStack() as whole:
        def sb(ctx, name, shape, dt=F32):
            return ctx.enter_context(nc.sbuf_tensor(name, shape, dt))

        def sem(name):
            return whole.enter_context(nc.semaphore(name))

        k_parts_rows = nc.dram_tensor("k_parts_rows", (B, PARTS, DK, H, S), BF16, kind="Internal").ap()
        q_parts_rows = nc.dram_tensor("q_parts_rows", (B, PARTS, DK, NC, H, CH), BF16, kind="Internal").ap()
        mask_rows = nc.dram_tensor("mask_rows", (B, E, S), BF16, kind="Internal").ap()
        xp_rows = nc.dram_tensor("xp_rows", (B, S, D), F32, kind="Internal").ap()
        attn_sums = nc.dram_tensor("attn_sums", (2, B, P, S), F32, kind="Internal").ap()

        bank = whole.enter_context(nc.psum_tensor("bank", [P, 8, CH], F32))

        X = sb(whole, "X", [P, B * NT, D])
        V = sb(whole, "V", [P, B * NT, D])
        ident = sb(whole, "ident", [P, P])
        wo = sb(whole, "wo", [P, D])
        bo_row = sb(whole, "bo_row", [P, D])
        gam_row = sb(whole, "gam_row", [P, D])
        beta_row = sb(whole, "beta_row", [P, D])
        coef = sb(whole, "coef", [P, 16])
        RED, BLUE, YELLOW, QSCALE, LN_EPS, OUT_FACTOR, DEN2, ROOT, TMP, GAM = (coef[:, i:i + 1] for i in range(10))

        scalars_in = sem("scalars_in")
        vectors_in = sem("vectors_in")
        weights_in = sem("weights_in")
        experts_in = sem("experts_in")
        x_in = [sem(f"x_in{b}") for b in range(B)]
        setup_done = sem("setup_done")
        q_scaled = sem("q_scaled")
        pe_ready = sem("pe_ready")
        centred = sem("centred")
        root_ready = sem("root_ready")
        var_ready = sem("var_ready")
        std_ready = sem("std_ready")
        angle_ready = sem("angle_ready")
        sine_ready = sem("sine_ready")
        dve_chain = sem("dve_chain")
        pool_chain = sem("pool_chain")
        xn_ready = sem("xn_ready")
        xp_ready = sem("xp_ready")
        xn_turned = sem("xn_turned")
        xp_turned = sem("xp_turned")
        xnT_ready = sem("xnT_ready")
        xpT_ready = sem("xpT_ready")
        gate_ready = sem("gate_ready")
        q_ready = sem("q_ready")
        k_ready = sem("k_ready")
        v_ready = sem("v_ready")
        xn_split = sem("xn_split")
        xp_stored = sem("xp_stored")
        q_read = sem("q_read")
        k_read = sem("k_read")
        v_read = sem("v_read")
        q_rest = sem("q_rest")
        k_rest = sem("k_rest")
        q_second = sem("q_second")
        k_second = sem("k_second")
        q_parts = sem("q_parts")
        k_parts = sem("k_parts")
        q_stored = sem("q_stored")
        k_stored = sem("k_stored")
        mask_ready = sem("mask_ready")
        mask_turned = sem("mask_turned")
        maskT_ready = sem("maskT_ready")
        mask_stored = sem("mask_stored")
        mask_spread = sem("mask_spread")
        prob_in = sem("prob_in")
        prob_exp = sem("prob_exp")
        high_ready = sem("high_ready")
        low_ready = sem("low_ready")
        hid_ready = sem("hid_ready")
        hid_relu = sem("hid_relu")
        hid_split = sem("hid_split")
        hid_used = sem("hid_used")
        sum_read = sem("sum_read")
        acc_ready = sem("acc_ready")
        acc_turned = sem("acc_turned")
        base_ready = sem("base_ready")
        beta_added = sem("beta_added")
        late_in = sem("late_in")
        ones_set = sem("ones_set")
        blank_ready = sem("blank_ready")
        pads_first = sem("pads_first")
        pads_rest = sem("pads_rest")
        unit_in = sem("unit_in")
        item_ready = sem("item_ready")
        item_read = sem("item_read")
        max_ready = sem("max_ready")
        max_turned = sem("max_turned")
        maxT_ready = sem("maxT_ready")
        maxT_parts = sem("maxT_parts")
        max_in = sem("max_in")
        logits_ready = sem("logits_ready")
        exp_out = sem("exp_out")
        v_staged = sem("v_staged")
        av_done = sem("av_done")
        sums_out = sem("sums_out")
        sums_stored = sem("sums_stored")
        sums_in = sem("sums_in")
        den_ready = sem("den_ready")
        outT_ready = sem("outT_ready")
        proj_ready = sem("proj_ready")
        proj_read = sem("proj_read")
        xpb_ready = sem("xpb_ready")
        y_ready = sem("y_ready")
        row_var = sem("row_var")
        row_std = sem("row_std")
        row_scale = sem("row_scale")
        result_ready = sem("result_ready")
        tail_chain = sem("tail_chain")
        result_out = sem("result_out")
        xp_in = sem("xp_in")

        def two_banks(i):
            return bank[:, i:i + 2, :].rearrange("p c s -> p (c s)")

        with ExitStack() as experts:
            W1H = sb(experts, "W1H", [P, E, F], F32R)
            W2H = sb(experts, "W2H", [P, E, F], F32R)
            W1L = sb(experts, "W1L", [P, E, F], F32R)
            W2L = sb(experts, "W2L", [P, E, F], F32R)
            B1 = sb(experts, "B1", [P, E, FT])
            B2 = sb(experts, "B2", [P, E])
            XTH = sb(experts, "XTH", [P, B * S], F32R)
            XTL = sb(experts, "XTL", [P, B * S], F32R)

            parts = sb(experts, "parts", [P, 2, PARTS, S], BF16)

            maskT = sb(experts, "maskT", [E, S], BF16)

            def store_parts(sp, b):
                sp.wait_ge(q_parts, b + 1)
                for n in range(PARTS):
                    for c in range(NC):
                        sp.dma_start(q_parts_rows[bass.ds(b, 1), n, :, c].rearrange("o d h s -> h (o d) s"),
                                     parts[:, 0, n, c * CH:(c + 1) * CH]).then_inc(q_stored, 16)
                sp.wait_ge(k_parts, b + 1)
                for n in range(PARTS):
                    sp.dma_start(k_parts_rows[bass.ds(b, 1), n].rearrange("o d h s -> h (o d) s"),
                                 parts[:, 1, n, :]).then_inc(k_stored, 16)

            with ExitStack() as one:
                wq, wk, wv = (sb(one, n, [P, D]) for n in ("wq", "wk", "wv"))
                gw = sb(one, "gw", [P, E])
                gb_row = sb(one, "gb_row", [P, E])
                bv_row = sb(one, "bv_row", [P, D])
                bqk = sb(one, "bqk", [P, 2])
                rden = sb(one, "rden", [P, D // 2])
                posc = sb(one, "posc", [P, NT])
                ang = sb(one, "ang", [P, NT, D // 2])
                turns_ = sb(one, "turns_", [P, NT, D // 2])
                pe_ = sb(one, "pe_", [P, NT, D])
                bn = sb(one, "bn", [P, B * NT, 6])
                mean_var = sb(one, "mean_var", [P, B * NT, 2])
                stat = sb(one, "stat", [P, 3, B * NT])
                FIRST, OTHERS = slice(0, NT), slice(NT, B * NT)
                var, std, rstd = (stat[:, i, :] for i in range(3))
                xc = sb(one, "xc", [P, NT, D])
                xs = sb(one, "xs", [P, NT, D])
                xnT = sb(one, "xnT", [P, S])
                xpT = sb(one, "xpT", [P, S])
                q32 = sb(one, "q32", [P, S])
                k32 = sb(one, "k32", [P, S])
                gate = sb(one, "gate", [P, 8, NT, E])
                few = sb(one, "few", [P, 8, NT])
                order = sb(one, "order", [P, E])
                mask = sb(one, "mask", [P, NT, E])
                raw = sb(one, "raw", [P, 2, E // B, F])
                half_sin = turns_

                def tiles(t, b):
                    return t[:, bass.ds(b * NT, NT), :]

                def spread(t):
                    return t.unsqueeze(2).to_broadcast([P, NT, E])

                ranks = order[:].unsqueeze(1).to_broadcast([P, NT, E])

                with nc.Block() as block:
                    @block.sync
                    def _(sp):
                        xv = x.rearrange("b (t p) d -> p (b t) d", p=P)
                        for b in range(B):
                            sp.dma_start(X[:, b * NT:(b + 1) * NT, :], xv[:, b * NT:(b + 1) * NT, :]).then_inc(x_in[b], 16)
                        for dst, src in ((ident[:], ident_in), (gw[:], gate_w), (wq[:], wqT), (wk[:], wkT), (wv[:], wvT)):
                            sp.dma_start(dst, src).then_inc(weights_in, 16)
                        for dst, src in ((B1[:], b1T), (B2[:], b2T), (wo[:], woT)):
                            sp.dma_start(dst, src).then_inc(late_in, 16)
                        def store_mask(b):
                            sp.wait_ge(maskT_ready, b + 1)
                            sp.dma_start(mask_rows[bass.ds(b, 1)].rearrange("o e s -> (o e) s"),
                                         maskT[:]).then_inc(mask_stored, 16)

                        def move(b, first=False, last=False):
                            if not first:
                                store_mask(b - 1)
                            if not last:
                                store_parts(sp, b)

                        move(0, first=True)
                        with sp.Fori(1, B - 1) as b:
                            move(b)
                        move(B - 1, last=True)
                        store_mask(B - 1)
                        sp.wait_ge(late_in, 3 * 16)
                        sp.wait_ge(xp_stored, B * 16)

                    @block.scalar
                    def _(act):
                        for dst, src in ((coef[:, 0:3], row(rby)), (rden[:], row(freq)), (posc[:], pos)):
                            act.dma_start(dst, src).then_inc(scalars_in, 16)
                        for dst, src in ((gam_row[:], row(gamma)), (beta_row[:], row(beta)), (bo_row[:], row(bo)),
                                         (bv_row[:], row(bv)), (gb_row[:], row(gate_b)), (order[:], row(rank_in)),
                                         (bqk[:, 0:1], bq), (bqk[:, 1:2], bk)):
                            act.dma_start(dst, src).then_inc(vectors_in, 16)
                        def root(rows):
                            nc.scalar.activation(std[:, rows], var[:, rows], ACT.Sqrt).then_inc(std_ready, 1)

                        act.wait_ge(var_ready, 1)
                        root(FIRST)
                        act.wait_ge(setup_done, 1)
                        nc.scalar.activation(ROOT, DEN2, ACT.Sqrt).then_inc(root_ready, 1)
                        act.wait_ge(angle_ready, 1)
                        nc.scalar.activation(pe_[:, :, 0:D:2], ang[:], ACT.Sin).then_inc(sine_ready, 1)
                        nc.scalar.activation(half_sin[:], ang[:], ACT.Sin, scale=0.5).then_inc(sine_ready, 1)
                        def high_parts(b):
                            act.wait_ge(experts_in, b * (3 * 16) + 3 * 16)
                            pair = bass.ds(b * (E // B), E // B)
                            nc.scalar.copy(W1H[:, pair, :], raw[:, 0]).then_inc(high_ready, 1)
                            nc.scalar.copy(W2H[:, pair, :], raw[:, 1]).then_inc(high_ready, 1)

                        def take_mask(b, first=False):
                            if not first:
                                act.wait_ge(mask_stored, b * 16)
                            act.wait_ge(mask_turned, b + 1)
                            nc.scalar.copy(maskT[:], bank[0:E, 4:6, :].rearrange("p c s -> p (c s)")).then_inc(maskT_ready, 1)

                        def front(b, first=False, second=False, ahead=True):
                            if not first:
                                act.wait_ge(gate_ready, b)
                                act.wait_ge(xn_split, b)
                            act.wait_ge(xn_turned, b + 1)
                            nc.scalar.copy(xnT[:], two_banks(0)).then_inc(xnT_ready, 1)
                            nc.scalar.copy(XTH[:, bass.ds(b * S, S)], two_banks(0)).then_inc(xnT_ready, 1)
                            act.wait_ge(xp_turned, b + 1)
                            nc.scalar.copy(xpT[:], two_banks(2)).then_inc(xpT_ready, 1)
                            act.wait_ge(xp_ready, b + 1)
                            act.dma_start(xp_rows[bass.ds(b, 1)].rearrange("o (t p) d -> p (o t) d", p=P),
                                          xs[:]).then_inc(xp_stored, 16)
                            if not first:
                                take_mask(b - 1, first=second)
                            act.wait_ge(prob_in, b + 1)
                            nc.scalar.activation(gate[:, 2], gate[:, 1], ACT.Exp).then_inc(prob_exp, 1)
                            act.wait_ge(q_scaled, 1)
                            if not first:
                                act.wait_ge(q_parts, b)
                                act.wait_ge(q_stored, b * (NC * PARTS_STORES))
                            act.wait_ge(q_ready, b + 1)
                            nc.scalar.activation(q32[:], two_banks(4), ACT.Identity, bias=bqk[:, 0:1],
                                                 scale=QSCALE).then_inc(q_read, 1)
                            nc.scalar.activation(parts[:, 0, 0, :], two_banks(4), ACT.Identity, bias=bqk[:, 0:1],
                                                 scale=QSCALE).then_inc(q_read, 1)
                            if not first:
                                act.wait_ge(k_parts, b)
                                act.wait_ge(k_stored, b * PARTS_STORES)
                            act.wait_ge(k_ready, b + 1)
                            nc.scalar.activation(k32[:], two_banks(0), ACT.Identity, bias=bqk[:, 1:2]).then_inc(k_read, 1)
                            nc.scalar.activation(parts[:, 1, 0, :], two_banks(0), ACT.Identity,
                                                 bias=bqk[:, 1:2]).then_inc(k_read, 1)
                            if ahead:
                                high_parts(b + 1)
                            act.wait_ge(q_rest, b + 1)
                            nc.scalar.copy(parts[:, 0, 1, :], q32[:]).then_inc(q_second, 1)
                            act.wait_ge(k_rest, b + 1)
                            nc.scalar.copy(parts[:, 1, 1, :], k32[:]).then_inc(k_second, 1)

                        high_parts(0)
                        act.wait_ge(var_ready, 2)
                        root(OTHERS)
                        front(0, first=True)
                        front(1, second=True)
                        with act.Fori(2, B - 1) as b:
                            front(b)
                        front(B - 1, ahead=False)
                        take_mask(B - 1)

                    @block.vector
                    def _(dve):
                        v = nc.vector
                        ch = Chain(dve, dve_chain)

                        def rows_statistics(b):
                            dve.wait_ge(x_in[b], 16)
                            for i in range(b * NT, (b + 1) * NT):
                                ch.done(v.bn_stats(bn[:, i, :], X[:, i, :]))

                        def variances(rows):
                            ch.settle()
                            for i in range(rows.start, rows.stop):
                                ch.done(v.bn_aggr(mean_var[:, i, :], bn[:, i, :]))
                            ch.settle()
                            v.tensor_scalar(var[:, rows], mean_var[:, rows, 1], 1e-5, None, ALU.add).then_inc(var_ready, 1)

                        def inverse_root(rows, count):
                            dve.wait_ge(std_ready, count)
                            r = rstd[:, rows]
                            ch.link(v.reciprocal(r, std[:, rows]))
                            ch.link(v.tensor_tensor(r, r, var[:, rows], ALU.mult))
                            ch.link(v.tensor_tensor(r, r, std[:, rows], ALU.add))
                            ch.link(v.tensor_scalar(r, r, 0.5, None, ALU.mult))
                            ch.link(v.reciprocal(r, r))

                        rows_statistics(0)
                        variances(FIRST)
                        dve.wait_ge(scalars_in, 3 * 16)
                        v.tensor_scalar(OUT_FACTOR, YELLOW, EPS_ADAPTIVE, 1.0, ALU.mult, ALU.add)
                        v.tensor_scalar(LN_EPS, BLUE, 0.1, 1.0, ALU.mult, ALU.add)
                        v.tensor_scalar(QSCALE, RED, 0.1, 1.0, ALU.mult, ALU.add)
                        v.tensor_scalar(GAM, RED, 0.1, 1.0, ALU.mult, ALU.add)
                        v.tensor_scalar(TMP, YELLOW, PHASE, 1.0, ALU.mult, ALU.add)
                        ch.link(v.tensor_scalar(DEN2, RED, TENSION, 1.0, ALU.mult, ALU.add))
                        v.tensor_scalar(LN_EPS, LN_EPS, 1e-5, None, ALU.mult)
                        v.scalar_tensor_tensor(QSCALE, BLUE, 0.05, QSCALE, ALU.mult, ALU.add)
                        v.scalar_tensor_tensor(GAM, YELLOW, 0.05, GAM, ALU.mult, ALU.add)
                        v.tensor_scalar(rden[:], rden[:], TMP, None, ALU.mult)
                        ch.link(v.tensor_scalar(DEN2, DEN2, float(DK), None, ALU.mult))
                        v.scalar_tensor_tensor(QSCALE, YELLOW, 0.15, QSCALE, ALU.mult, ALU.add).then_inc(setup_done, 1)
                        ch.link(v.reciprocal(rden[:], rden[:]))
                        ch.link(v.tensor_tensor(ang[:], posc[:].unsqueeze(2).to_broadcast([P, NT, D // 2]),
                                                rden[:].unsqueeze(1).to_broadcast([P, NT, D // 2]), ALU.mult))
                        ch.link(v.tensor_scalar(turns_[:], ang[:], 0.5 / PI, ROUND, ALU.mult, ALU.add))
                        ch.link(v.tensor_scalar(turns_[:], turns_[:], ROUND, None, ALU.subtract))
                        ch.link(v.scalar_tensor_tensor(ang[:], turns_[:], -TWO_PI_HI, ang[:], ALU.mult, ALU.add))
                        ch.link(v.scalar_tensor_tensor(ang[:], turns_[:], -TWO_PI_LO, ang[:], ALU.mult, ALU.add))
                        v.tensor_scalar(ang[:], ang[:], -PI_DOWN, PI_DOWN, ALU.max, ALU.min).then_inc(angle_ready, 1)
                        dve.wait_ge(root_ready, 1)
                        ch.link(v.reciprocal(TMP, ROOT))
                        ch.link(v.scalar_tensor_tensor(TMP, TMP, DEN2, ROOT, ALU.mult, ALU.add))
                        ch.link(v.tensor_scalar(TMP, TMP, 0.5, None, ALU.mult))
                        ch.link(v.reciprocal(TMP, TMP))
                        ch.link(v.tensor_scalar(QSCALE, QSCALE, TMP, None, ALU.mult))
                        dve.wait_ge(vectors_in, 8 * 16)
                        v.tensor_scalar(gam_row[:], gam_row[:], GAM, None, ALU.mult)
                        v.tensor_scalar(bqk[:, 0:1], bqk[:, 0:1], QSCALE, None, ALU.mult).then_inc(q_scaled, 1)

                        dve.wait_ge(sine_ready, 2)
                        ch.link(v.tensor_tensor(half_sin[:], half_sin[:], half_sin[:], ALU.mult))
                        v.tensor_scalar(pe_[:, :, 1:D:2], half_sin[:], -2.0, 1.0, ALU.mult, ALU.add).then_inc(pe_ready, 1)
                        inverse_root(FIRST, 1)

                        def normalise(b, first=False):
                            if not first:
                                dve.wait_ge(xn_turned, b)
                                dve.wait_ge(xp_ready, b)
                            at = bass.ds(b * NT, NT)
                            v.tensor_tensor(xc[:], tiles(X, b), mean_var[:, at, 0:1].to_broadcast([P, NT, D]),
                                            ALU.subtract).then_inc(centred, 1)
                            dve.wait_ge(centred, b + 1)
                            v.tensor_tensor(xc[:], xc[:], stat[:, 2, at].unsqueeze(2).to_broadcast([P, NT, D]),
                                            ALU.mult).then_inc(xn_ready, 1)

                        GATE_STEPS = 16

                        def front(b, first=False, ahead=True):
                            dve.wait_ge(xnT_ready, 2 * b + 2)
                            v.tensor_tensor(XTL[:, bass.ds(b * S, S)], xnT[:], XTH[:, bass.ds(b * S, S)].bitcast(F32),
                                            ALU.subtract).then_inc(xn_split, 1)
                            dve.wait_ge(gate_ready, b + 1)
                            ch.link(v.tensor_tensor(gate[:, 0], bank[:, 7, 0:NT * E].rearrange("p (t e) -> p t e", e=E),
                                                    gb_row[:].unsqueeze(1).to_broadcast([P, NT, E]), ALU.add))
                            ch.link(v.tensor_reduce(few[:, 0], gate[:, 0], AX_X, ALU.max))
                            v.tensor_tensor(gate[:, 1], gate[:, 0], spread(few[:, 0]), ALU.subtract).then_inc(prob_in, 1)
                            if ahead:
                                normalise(b + 1)
                            dve.wait_ge(prob_exp, b + 1)
                            ch.link(v.tensor_reduce(few[:, 1], gate[:, 2], AX_X, ALU.add))
                            ch.link(v.reciprocal(few[:, 1], few[:, 1]))
                            ch.link(v.tensor_tensor(gate[:, 3], gate[:, 2], spread(few[:, 1]), ALU.mult))
                            ch.link(v.tensor_reduce(few[:, 2], gate[:, 3], AX_X, ALU.max))
                            ch.link(v.tensor_tensor(gate[:, 4], gate[:, 3], spread(few[:, 2]), ALU.is_equal))
                            ch.link(v.tensor_tensor(gate[:, 4], gate[:, 4], ranks, ALU.mult))
                            ch.link(v.tensor_reduce(few[:, 3], gate[:, 4], AX_X, ALU.max))
                            ch.link(v.tensor_tensor(gate[:, 5], ranks, spread(few[:, 3]), ALU.is_equal))
                            ch.link(v.scalar_tensor_tensor(gate[:, 3], gate[:, 5], -2.0, gate[:, 3], ALU.mult, ALU.add))
                            ch.link(v.tensor_reduce(few[:, 4], gate[:, 3], AX_X, ALU.max))
                            ch.link(v.tensor_tensor(gate[:, 4], gate[:, 3], spread(few[:, 4]), ALU.is_equal))
                            ch.link(v.tensor_tensor(gate[:, 4], gate[:, 4], ranks, ALU.mult))
                            ch.link(v.tensor_reduce(few[:, 5], gate[:, 4], AX_X, ALU.max))
                            ch.link(v.tensor_tensor(gate[:, 6], ranks, spread(few[:, 5]), ALU.is_equal))
                            if not first:
                                dve.wait_ge(mask_turned, b)
                            v.tensor_tensor(mask[:], gate[:, 5], gate[:, 6], ALU.add).then_inc(mask_ready, 1)
                            dve.wait_ge(v_ready, b + 1)
                            v.tensor_tensor(tiles(V, b), two_banks(2).rearrange("p (t d) -> p t d", d=D),
                                            bv_row[:].unsqueeze(1).to_broadcast([P, NT, D]), ALU.add).then_inc(v_read, 1)
                            dve.wait_ge(q_read, 2 * b + 2)
                            v.tensor_tensor(q32[:], q32[:], parts[:, 0, 0, :], ALU.subtract).then_inc(q_rest, 1)
                            dve.wait_ge(q_second, b + 1)
                            v.tensor_tensor(parts[:, 0, 2, :], q32[:], parts[:, 0, 1, :],
                                            ALU.subtract).then_inc(q_parts, 1)

                        normalise(0, first=True)
                        for b in range(1, B):
                            rows_statistics(b)
                        variances(OTHERS)
                        inverse_root(OTHERS, 2)
                        dve.wait_ge(late_in, 3 * 16)
                        v.tensor_scalar(wo[:], wo[:], OUT_FACTOR, None, ALU.mult)
                        front(0, first=True)
                        with dve.Fori(1, B - 1) as b:
                            ch.turn(b - 1, GATE_STEPS)
                            front(b)
                            ch.end_turns(B - 2)
                        front(B - 1, ahead=False)

                    @block.gpsimd
                    def _(pool):
                        tt = nc.gpsimd.tensor_tensor

                        def load_weights(b):
                            if not (isinstance(b, int) and b == 0):
                                pool.wait_ge(low_ready, 2 * b)
                            pair = bass.ds(b * (E // B), E // B)
                            pool.dma_start(raw[:, 0], w1[pair].rearrange("e d f -> d e f")).then_inc(experts_in, 16)
                            for i in range(E // B):
                                pool.dma_start(raw[:, 1, i, :].rearrange("p (t d) -> p t d", d=D),
                                               w2[bass.ds(b * (E // B) + i, 1)].rearrange(
                                                   "o (t p) d -> p (o t) d", p=P)).then_inc(experts_in, 16)

                        def low_parts(b, last=False):
                            pool.wait_ge(high_ready, 2 * b + 2)
                            pair = bass.ds(b * (E // B), E // B)
                            tt(W1L[:, pair, :], raw[:, 0], W1H[:, pair, :].bitcast(F32), ALU.subtract).then_inc(low_ready, 1)
                            tt(W2L[:, pair, :], raw[:, 1], W2H[:, pair, :].bitcast(F32), ALU.subtract).then_inc(low_ready, 1)
                            if not last:
                                load_weights(b + 1)

                        def encode(b, first=False):
                            pool.wait_ge(xn_ready, b + 1)
                            if not first:
                                pool.wait_ge(xp_turned, b)
                                pool.wait_ge(xp_stored, b * 16)
                            tt(xs[:], xc[:], pe_[:], ALU.add).then_inc(xp_ready, 1)

                        def front(b, ahead=True, last=False):
                            if ahead:
                                encode(b + 1)
                            pool.wait_ge(k_read, 2 * b + 2)
                            tt(k32[:], k32[:], parts[:, 1, 0, :], ALU.subtract).then_inc(k_rest, 1)
                            pool.wait_ge(k_second, b + 1)
                            tt(parts[:, 1, 2, :], k32[:], parts[:, 1, 1, :], ALU.subtract).then_inc(k_parts, 1)
                            if ahead:
                                low_parts(b + 1, last)

                        load_weights(0)
                        pool.wait_ge(pe_ready, 1)
                        encode(0, first=True)
                        low_parts(0)
                        with pool.Fori(0, B - 2) as b:
                            front(b)
                        front(B - 2, last=True)
                        front(B - 1, ahead=False)

                    @block.tensor
                    def _(pe):
                        mm, turned = nc.tensor.matmul, nc.tensor.transpose
                        pe.wait_ge(weights_in, 5 * 16)

                        def turn_mask(b):
                            pe.wait_ge(q_read, 2 * b + 2)
                            pe.wait_ge(mask_ready, b + 1)
                            for t in range(NT):
                                last = turned(bank[0:E, 4 + t // 4, (t % 4) * P:(t % 4 + 1) * P], mask[:, t, :], ident[:])
                            last.then_inc(mask_turned, 1)

                        def front(b, first=False):
                            if not first:
                                pe.wait_ge(k_read, 2 * b)
                            pe.wait_ge(xn_ready, b + 1)
                            for t in range(NT):
                                last = turned(bank[:, t // 4, (t % 4) * P:(t % 4 + 1) * P], xc[:, t, :], ident[:])
                            last.then_inc(xn_turned, 1)
                            if not first:
                                pe.wait_ge(v_read, b)
                            pe.wait_ge(xp_ready, b + 1)
                            for t in range(NT):
                                last = turned(bank[:, 2 + t // 4, (t % 4) * P:(t % 4 + 1) * P], xs[:, t, :], ident[:])
                            last.then_inc(xp_turned, 1)
                            if not first:
                                turn_mask(b - 1)
                            pe.wait_ge(xnT_ready, 2 * b + 1)
                            for t in range(NT):
                                last = mm(bank[:, 7, t * E:(t + 1) * E], xnT[:, t * P:(t + 1) * P], gw[:],
                                          start=True, stop=True)
                            last.then_inc(gate_ready, 1)
                            pe.wait_ge(xpT_ready, b + 1)
                            if not first:
                                pe.wait_ge(maskT_ready, b)
                            for c in range(NC):
                                last = mm(bank[:, 4 + c, :], wq[:], xpT[:, c * CH:(c + 1) * CH], start=True, stop=True)
                            last.then_inc(q_ready, 1)
                            for c in range(NC):
                                last = mm(bank[:, c, :], wk[:], xpT[:, c * CH:(c + 1) * CH], start=True, stop=True)
                            last.then_inc(k_ready, 1)
                            for t in range(NT):
                                last = mm(bank[:, 2 + t // 4, (t % 4) * P:(t % 4 + 1) * P], xpT[:, t * P:(t + 1) * P], wv[:],
                                          start=True, stop=True)
                            last.then_inc(v_ready, 1)

                        front(0, first=True)
                        with pe.Fori(1, B) as b:
                            front(b)
                        turn_mask(B - 1)
            HIDDEN = (0, 1, 6, 7)
            CREDIT_SPLIT, CREDIT_USED, CREDIT_RELU, CREDIT_SUM, CREDIT_BASE = 2, 4, 8, 2, 1
            with ExitStack() as one:
                mask_all = sb(one, "mask_all", [P, 2, E, CH], BF16)
                hid = sb(one, "hid", [P, 2, CH])
                HH = sb(one, "HH", [P, FT, CH], F32R)
                HL = sb(one, "HL", [P, FT, CH], F32R)
                masked = sb(one, "masked", [P, 2, CH])
                acc = sb(one, "acc", [P, CH])

                with nc.Block() as block:
                    @block.sync
                    def _(sp):
                        def load_mask(c):
                            b, half = c >> 1, c & 1
                            if not isinstance(c, int):
                                b = b & (B - 1)
                                sp.compute_val(b)
                                sp.compute_val(half)
                                sp.wait_ge(mask_spread, c * 16)
                                sp.wait_ge(sum_read, (c - 1) * E + CREDIT_SUM)
                            elif c:
                                sp.wait_ge(mask_spread, c * 16)
                            sp.dma_start(mask_all[:, bass.ds(half, 1)].rearrange("p o e s -> p (o e) s"),
                                         mask_rows[bass.ds(b, 1), :, bass.ds(half * CH, CH)].rearrange(
                                             "o e s -> (o e) s").partition_broadcast(P)).then_inc(mask_spread, 16)

                        sp.wait_ge(mask_stored, B * 16)
                        load_mask(0)
                        load_mask(1)
                        store_parts(sp, B - 1)
                        with sp.Fori(2, CHUNKS) as c:
                            load_mask(c)
                        sp.wait_ge(mask_spread, CHUNKS * 16)
                        sp.wait_ge(q_stored, B * (NC * PARTS_STORES))
                        sp.wait_ge(k_stored, B * PARTS_STORES)

                    @block.scalar
                    def _(act):
                        with act.Fori(0, CHUNKS) as c:
                            for j in range(TILES):
                                e, t, n = j // FT, j % FT, c * TILES + j
                                act.wait_ge(hid_ready, n + 1)
                                act.wait_ge(hid_split, n - 1 + CREDIT_SPLIT)
                                act.wait_ge(hid_used, n - 3 + CREDIT_USED)
                                nc.scalar.activation(hid[:, j % 2, :], bank[:, HIDDEN[t], :], ACT.Relu,
                                                     bias=B1[:, e, t:t + 1]).then_inc(hid_relu, 1)
                                nc.scalar.activation(HH[:, t, :], bank[:, HIDDEN[t], :], ACT.Relu,
                                                     bias=B1[:, e, t:t + 1]).then_inc(hid_relu, 1)

                    @block.vector
                    def _(dve):
                        v = nc.vector
                        v.memset(masked[:, 0, 0:1], 0.0).then_inc(hid_split, CREDIT_SPLIT)
                        v.memset(masked[:, 0, 1:2], 0.0).then_inc(hid_used, CREDIT_USED)
                        v.memset(masked[:, 0, 2:3], 0.0).then_inc(hid_relu, CREDIT_RELU)
                        v.memset(masked[:, 0, 3:4], 0.0).then_inc(sum_read, CREDIT_SUM)
                        v.memset(masked[:, 0, 4:5], 0.0).then_inc(base_ready, CREDIT_BASE)

                        def split(c, j):
                            n = c * TILES + j
                            dve.wait_ge(hid_relu, 2 * n + 2 + CREDIT_RELU)
                            v.tensor_tensor(HL[:, j % FT, :], hid[:, j % 2, :], HH[:, j % FT, :].bitcast(F32),
                                            ALU.subtract).then_inc(hid_split, 1)

                        def take(c, e, first=False):
                            n = c * E + e
                            dve.wait_ge(hid_used, n * FT + FT + CREDIT_USED)
                            if e == 0:
                                dve.wait_ge(mask_spread, c * 16 + 16)
                                if not first:
                                    dve.wait_ge(acc_turned, c)
                            dst = acc[:] if e == 0 else masked[:, e % 2, :]
                            v.scalar_tensor_tensor(dst, bank[:, 2 + e % 2, :], B2[:, e:e + 1],
                                                   mask_all[:, bass.ds(c & 1, 1), e, :].rearrange("p o s -> p (o s)"),
                                                   ALU.add, ALU.mult).then_inc(sum_read, 1)

                        def add(c, e):
                            dve.wait_ge(sum_read, c * E + e + 1 + CREDIT_SUM)
                            if e > 1:
                                dve.wait_ge(acc_ready, c * (E - 1) + e - 1)
                            v.tensor_tensor(acc[:], acc[:], masked[:, e % 2, :], ALU.add).then_inc(acc_ready, 1)

                        def give(c):
                            dve.wait_ge(acc_turned, c + 1)
                            xt = X[:, bass.ds(c * (NT // NC), NT // NC), :]
                            v.tensor_tensor(xt, xt, bank[:, 5, :].rearrange("p (t d) -> p t d", d=D),
                                            ALU.add).then_inc(base_ready, 1)

                        def chunk(c, first=False):
                            for j in range(TILES):
                                e = j // FT
                                split(c, j)
                                if j % FT == 2 and e:
                                    take(c, e - 1, first)
                                if j % FT == 3 and e > 1:
                                    add(c, e - 1)
                                if not first and j == 2:
                                    take(c - 1, E - 1)
                                if not first and j == 3:
                                    add(c - 1, E - 1)
                                if not first and j == 7:
                                    give(c - 1)

                        chunk(0, first=True)
                        dve.wait_ge(beta_added, B)
                        with dve.Fori(1, CHUNKS) as c:
                            chunk(c)
                        take(CHUNKS - 1, E - 1)
                        add(CHUNKS - 1, E - 1)
                        give(CHUNKS - 1)

                    @block.gpsimd
                    def _(pool):
                        for b in range(B):
                            xt = X[:, b * NT:(b + 1) * NT, :]
                            nc.gpsimd.tensor_tensor(xt, xt, beta_row[:].unsqueeze(1).to_broadcast([P, NT, D]),
                                                    ALU.add).then_inc(beta_added, 1)

                    @block.tensor
                    def _(pe):
                        mm, turned = nc.tensor.matmul, nc.tensor.transpose

                        def first_weights(c, j):
                            e, t, n = j // FT, j % FT, c * TILES + j
                            pe.wait_ge(hid_relu, 2 * (n - 3) + CREDIT_RELU)
                            dst, cols, at = bank[:, HIDDEN[t], :], slice(t * P, (t + 1) * P), bass.ds(c * CH, CH)
                            mm(dst, W1H[:, e, cols], XTH[:, at], start=True, stop=False)
                            mm(dst, W1H[:, e, cols], XTL[:, at], start=False, stop=False)
                            mm(dst, W1L[:, e, cols], XTH[:, at], start=False, stop=True).then_inc(hid_ready, 1)

                        def second_weights(c, j):
                            e, t = j // FT, j % FT
                            if t == 0:
                                pe.wait_ge(sum_read, c * E + e - 1 + CREDIT_SUM)
                            pe.wait_ge(hid_split, c * TILES + j + 1 + CREDIT_SPLIT)
                            dst, cols = bank[:, 2 + e % 2, :], slice(t * P, (t + 1) * P)
                            mm(dst, W2H[:, e, cols], HH[:, t, :], start=(t == 0), stop=False)
                            mm(dst, W2H[:, e, cols], HL[:, t, :], start=False, stop=False)
                            last = mm(dst, W2L[:, e, cols], HH[:, t, :], start=False, stop=(t == FT - 1))
                            last.then_inc(hid_used, 1)

                        def turn(c):
                            pe.wait_ge(acc_ready, c * (E - 1) + E - 1)
                            pe.wait_ge(base_ready, c + CREDIT_BASE)
                            for t in range(NT // NC):
                                last = turned(bank[:, 5, t * P:(t + 1) * P], acc[:, t * P:(t + 1) * P], ident[:])
                            last.then_inc(acc_turned, 1)

                        def chunk(c, first=False):
                            for j in range(TILES):
                                first_weights(c, j)
                                if j >= LAG:
                                    second_weights(c, j - LAG)
                                elif not first:
                                    second_weights(c - 1, TILES + j - LAG)
                                if j == 5 and not first:
                                    turn(c - 1)

                        chunk(0, first=True)
                        with pe.Fori(1, CHUNKS) as c:
                            chunk(c)
                        second_weights(CHUNKS - 1, TILES - 2)
                        second_weights(CHUNKS - 1, TILES - 1)
                        turn(CHUNKS - 1)

        STEPS = NT
        PROJECT_STEP, ROOT_STEP = 7, 6
        CREDIT_RESULT = 1

        def TAIL(b):
            return (b + 1) * (NG * NC) + 1

        TURNED = 2
        NARROW = (4, 5, 7)
        WIDE = (4, 5, 7, 0)

        def logits_bank(t, u, wide):
            return bank[:, WIDE[u] if wide else NARROW[(t * U + u) % len(NARROW)], :]

        CREDIT_AV, CREDIT_EXP, CREDIT_ITEM, CREDIT_PAIR, CREDIT_TURNED = STEPS, 2, 2, 1, 1
        CREDIT_MAX, CREDIT_SUMS = PARTS * 16, 2 * U * 16
        UC = U * S
        LOADS = PARTS + PARTS * NC
        CREDIT_UNIT = LOADS * 16
        tail = whole.enter_context(ExitStack())
        XP = sb(tail, "XP", [P, B * NT, D])
        numer = sb(tail, "numer", [P, S])
        denom = sb(tail, "denom", [P, S])
        outT = sb(tail, "outT", [P, S])
        y = sb(tail, "y", [P, NT, D])
        result = sb(tail, "result", [P, NT, D])
        bn2 = sb(tail, "bn2", [P, NT, 6])
        mean_var2 = sb(tail, "mean_var2", [P, NT, 2])
        spare = sb(tail, "spare", [P, 1])
        v8, s8, r8 = (sb(tail, n, [P, NT]) for n in ("v8", "s8", "r8"))
        out_tiles = out.rearrange("b (t p) d -> p (b t) d", p=P)

        HT, LAST = NT // 2, B - 1

        def half_of(t, h):
            return t[:, h * HT:(h + 1) * HT]

        def over_rows(t):
            return t[:].unsqueeze(1).to_broadcast([P, NT, D])

        def over_channels(t):
            return t.unsqueeze(2).to_broadcast([P, NT, D])

        with ExitStack() as two:
            QS = sb(two, "QS", [KR2, RING * UC], BF16)
            KS = sb(two, "KS", [KR2, RING * UC], BF16)
            probs = sb(two, "probs", [P, 2, U, CH])
            VS = sb(two, "VS", [P, STEPS, U, 32])
            row_max = sb(two, "row_max", [P, 2, ITEMS])
            neg_max = sb(two, "neg_max", [P, ITEMS])
            maxT = sb(two, "maxT", [ITEMS, P])
            zeros = sb(two, "zeros", [ITEMS, P])
            max_rest = sb(two, "max_rest", [ITEMS, P])
            max_parts = sb(two, "max_parts", [ITEMS, PARTS, P], BF16)
            sums = sb(two, "sums", [P, 2, CH])
            blank = sb(two, "blank", [KR - PROD, S], BF16)
            one_row = sb(two, "one_row", [PARTS, S], BF16)

            with nc.Block() as block:
                @block.sync
                def _(sp):
                    def ahead(*values):
                        for value in values:
                            if not isinstance(value, int):
                                sp.compute_val(value)

                    def place(u):
                        slot, b, g = u & (RING - 1), (u >> 2) & (B - 1), u & (NG - 1)
                        ahead(slot, b, g)
                        return slot, b, g

                    def load_unit(u):
                        slot, b, g = place(u)
                        heads = bass.ds(g * U, U)
                        cols = bass.ds(slot * UC, UC)
                        sp.wait_ge(unit_in, u * (LOADS * 16) + CREDIT_UNIT)
                        for i in range(PARTS):
                            rows = slice(i * PARTS * DK, (i + 1) * PARTS * DK)
                            sp.dma_start(KS[rows, cols], k_parts_rows[bass.ds(b, 1), :, :, heads, :].rearrange(
                                "o n d u s -> (o n d) (u s)")).then_inc(unit_in, 16)
                            for c in range(NC):
                                q = q_parts_rows[bass.ds(b, 1), i, :, c, heads, :].rearrange("o d u s -> (o d) (u s)")
                                sp.dma_start(QS[rows, bass.ds(slot * UC + c * HALF, HALF)],
                                             q.unsqueeze(0).to_broadcast([PARTS, DK, HALF])).then_inc(unit_in, 16)

                    def load_max(v):
                        slot = v & (2 * RING - 1)
                        ahead(slot)
                        sp.wait_ge(maxT_parts, v + 2)
                        sp.wait_ge(max_in, v * (PARTS * 16) + CREDIT_MAX)
                        for n in range(PARTS):
                            sp.dma_start(QS[KR + n:KR + n + 1, bass.ds(slot * HALF, HALF)],
                                         max_parts[:, n, :]).then_inc(max_in, 16)

                    def store_sums(w):
                        b, g, c = (w >> 3) & (B - 1), (w >> 1) & (NG - 1), w & (NC - 1)
                        ahead(b, g, c)
                        sp.wait_ge(sums_out, w + 1 + CREDIT_PAIR)
                        sp.wait_ge(sums_stored, w * (U * 16) + CREDIT_SUMS)
                        for u in range(U):
                            dst = attn_sums[:, bass.ds(b, 1), bass.ds(g * (U * DK) + u * DK, DK), bass.ds(c * CH, CH)]
                            sp.dma_start(dst.rearrange("m o d q -> (m o) d q"),
                                         sums[32 * u:32 * u + 2 * DK, bass.ds(c, 1), :]).then_inc(sums_stored, 16)

                    with sp.Fori(0, RING) as u:
                        load_unit(u)
                    sp.dma_start(XP[:], xp_rows.rearrange("b (t p) d -> p (b t) d", p=P)).then_inc(xp_in, 16)
                    with sp.Fori(0, LEAD) as v:
                        load_max(v)
                    load_max(LEAD)
                    def unit(u, last_of=None):
                        store_sums(2 * u)
                        load_max(2 * u + (LEAD + 1))
                        store_sums(2 * u + 1)
                        place(u + RING)
                        sp.wait_ge(av_done, u * (NC * STEPS) + (NC * STEPS + CREDIT_AV))
                        if last_of is not None:
                            load_sums(last_of)
                        load_unit(u + RING)
                        load_max(2 * u + (LEAD + 2))

                    def load_sums(b):
                        sp.wait_ge(sums_stored, (b + 1) * (NG * NC * U * 16) + CREDIT_SUMS)
                        for m, dst in ((1, denom), (0, numer)):
                            sp.dma_start(dst[:], attn_sums[m, bass.ds(b, 1)].rearrange("o p s -> (o p) s")).then_inc(sums_in, 16)

                    def store_result(b):
                        sp.wait_ge(result_ready, b + 1 + CREDIT_RESULT)
                        sp.dma_start(out_tiles[:, bass.ds(b * NT, NT), :], result[:]).then_inc(result_out, 16)

                    def batch(b, first=False):
                        for g in range(NG):
                            unit(b * NG + g, last_of=b if g == NG - 1 else None)
                            if g == 2 and not first:
                                store_result(b - 1)

                    assert NU - RING == (B - 1) * NG
                    batch(0, first=True)
                    with sp.Fori(1, B - 1) as b:
                        batch(b)
                    with sp.Fori(2 * (NU - RING), NW - LEAD - 1) as w:
                        store_sums(w)
                        load_max(w + (LEAD + 1))
                    with sp.Fori(NW - LEAD - 1, NW - 2) as w:
                        store_sums(w)
                    store_result(B - 2)
                    for c in range(NC):
                        store_sums(NW - NC + c)
                        sp.wait_ge(sums_stored, (NW - NC + c + 1) * (U * 16) + CREDIT_SUMS)
                        if c:
                            sp.wait_ge(sums_in, (B - 1 + c) * 32)
                        for m, dst in ((1, denom), (0, numer)):
                            sp.dma_start(dst[:, c * CH:(c + 1) * CH],
                                         attn_sums[m, B - 1, :, c * CH:(c + 1) * CH]).then_inc(sums_in, 16)
                    for h in range(2):
                        sp.wait_ge(result_ready, B + h + CREDIT_RESULT)
                        if h == 0:
                            sp.wait_ge(result_out, (B - 1) * 16)
                        sp.dma_start(out_tiles[:, LAST * NT + h * HT:LAST * NT + (h + 1) * HT, :],
                                     half_of(result, h)).then_inc(result_out, 16)
                    sp.wait_ge(result_out, (B + 1) * 16)

                @block.tensor
                def _(pe):
                    mm = nc.tensor.matmul

                    def max_item(i, v, turned=None):
                        if i == 0:
                            pe.wait_ge(unit_in, (v >> 1) * (LOADS * 16) + (LOADS * 16 + CREDIT_UNIT))
                        if i == turned:
                            pe.wait_ge(maxT_ready, v + CREDIT_TURNED)
                        pe.wait_ge(item_read, v * ITEMS + (i - 1 + CREDIT_ITEM))
                        at = ((v >> 1) & (RING - 1)) * UC + (i // (NT // NC)) * S
                        for c in range(NC):
                            last = mm(bank[:, 2 * (i % 2) + c, :], QS[0:KR, bass.ds((v & (2 * RING - 1)) * HALF + i * P, P)],
                                      KS[0:KR, bass.ds(at + c * CH, CH)], start=True, stop=True)
                        last.then_inc(item_ready, 1)

                    def turn_max(v, items):
                        pe.wait_ge(max_ready, v + 1)
                        if items:
                            pe.wait_ge(item_read, (v + 1) * ITEMS + (items + CREDIT_ITEM))
                        nc.tensor.transpose(bank[0:ITEMS, TURNED, 0:P], neg_max[:], ident[:]).then_inc(max_turned, 1)

                    def logits(w, t, u, wide=False, after_narrow=False):
                        if t == 0 and u == 0:
                            pe.wait_ge(max_in, w * (PARTS * 16) + (PARTS * 16 + CREDIT_MAX))
                        if wide:
                            back = 2 if after_narrow and t == 0 else U
                        else:
                            back = 2 if t == 0 and u < 2 else len(NARROW)
                        pe.wait_ge(exp_out, w * (STEPS * U) + (t * U + u + 1 - back + CREDIT_EXP))
                        at = ((w >> 1) & (RING - 1)) * UC + u * S
                        mm(logits_bank(t, u, wide), KS[:, bass.ds(at + t * P, P)],
                           QS[:, bass.ds((w & (2 * RING - 1)) * HALF + u * CH, CH)], start=True, stop=True).then_inc(logits_ready, 1)

                    def product(w, t):
                        if t == 0:
                            pe.wait_ge(sums_out, w + CREDIT_PAIR)
                        pe.wait_ge(v_staged, (w >> 1) * STEPS + (t + 1))
                        pe.wait_ge(exp_out, w * (STEPS * U) + (t * U + U + CREDIT_EXP))
                        for u in range(U):
                            last = mm(bank[32 * u:32 * u + 32, 6, :], VS[:, t, u, :], probs[:, t % 2, u, :],
                                      start=(t == 0), stop=(t == STEPS - 1))
                        last.then_inc(av_done, 1)

                    def project(b):
                        pe.wait_ge(outT_ready, b + 1)
                        for t in range(NT):
                            last = mm(bank[:, 2 + t // 4, (t % 4) * P:(t % 4 + 1) * P],
                                      outT[:, t * P:(t + 1) * P], wo[:], start=True, stop=True)
                        last.then_inc(proj_ready, 1)

                    def pair(w, items=True, turn=True, before=True, tail_of=None):
                        wide = dict(wide=not items, after_narrow=turn)
                        if not items and turn:
                            pe.wait_ge(item_read, NW * ITEMS + CREDIT_ITEM)
                        def last_product(t):
                            if t:
                                product(w, t - 1)
                            elif before:
                                product(w - 1, STEPS - 1)

                        for t in range(STEPS):
                            if items:
                                max_item(2 * t, w + LEAD)
                            logits(w, t, 0, **wide)
                            logits(w, t, 1, **wide)
                            if items:
                                last_product(t)
                            if turn and t == 1:
                                turn_max(w + (LEAD - 1), 2 if items else 0)
                            if tail_of is not None and t == PROJECT_STEP:
                                pe.wait_ge(item_read, (w + LEAD) * ITEMS + (2 * t + CREDIT_ITEM))
                                project(tail_of)
                            logits(w, t, 2, **wide)
                            logits(w, t, 3, **wide)
                            if tail_of is not None and t == PROJECT_STEP:
                                pe.wait_ge(proj_read, tail_of + 1)
                            if not items:
                                last_product(t)
                            if items:
                                max_item(2 * t + 1, w + LEAD, turned=3)

                    pe.wait_ge(pads_first, 2 * 16)
                    for i in range(ITEMS):
                        max_item(i, 0)
                    pe.wait_ge(pads_rest, 3 * 16)
                    with pe.Fori(1, LEAD) as v:
                        for i in range(ITEMS):
                            max_item(i, v, turned=5)
                            if i == 3:
                                turn_max(v - 1, 4)
                    pair(0, before=False)
                    with pe.Fori(0, 4) as i:
                        pair(2 * i + 1)
                        pair(2 * i + 2)
                    with pe.Fori(0, B - 2) as b:
                        pair(TAIL(b), tail_of=b)
                        pair(TAIL(b) + 1)
                        with pe.Fori(0, 3) as i:
                            pair(TAIL(b) + 2 * i + 2)
                            pair(TAIL(b) + 2 * i + 3)
                    pair(TAIL(B - 2), tail_of=B - 2)
                    for w in range(TAIL(B - 2) + 1, NW - LEAD):
                        pair(w)
                    pair(NW - LEAD, items=False)
                    with pe.Fori(NW - LEAD + 1, NW) as w:
                        pair(w, items=False, turn=False)

                    def project_half(h):
                        pe.wait_ge(outT_ready, B + h)
                        for t in range(HT):
                            last = mm(bank[:, 2 + h, t * P:(t + 1) * P], outT[:, (h * HT + t) * P:(h * HT + t + 1) * P],
                                      wo[:], start=True, stop=True)
                        last.then_inc(proj_ready, 1)

                    product(NW - 1, STEPS - 1)
                    project_half(0)
                    project_half(1)

                @block.scalar
                def _(act):
                    def pad(dst, src, signal):
                        rows, times = src.shape[0], dst.shape[1] // S
                        act.dma_start(dst.rearrange("p (n s) -> p n s", s=S),
                                      src[:].unsqueeze(1).to_broadcast([rows, times, S])).then_inc(signal, 16)

                    act.wait_ge(blank_ready, 2)
                    for operand in (KS, QS):
                        pad(operand[PROD:KR, 0:UC], blank, pads_first)
                    for operand in (KS, QS):
                        pad(operand[PROD:KR, UC:RING * UC], blank, pads_rest)
                    pad(KS[KR:KR2, :], one_row, pads_rest)
                    def take_turned(v):
                        act.wait_ge(max_turned, v + 1)
                        act.wait_ge(maxT_parts, v + 1)
                        nc.scalar.copy(maxT[:], bank[0:ITEMS, TURNED, 0:P]).then_inc(maxT_ready, 1)

                    def take_sums(w):
                        act.wait_ge(av_done, w * STEPS + (STEPS + CREDIT_AV))
                        act.wait_ge(sums_stored, w * (U * 16) + CREDIT_SUMS - U * 16)
                        nc.scalar.copy(sums[:, bass.ds(w & 1, 1), :].rearrange("p o q -> p (o q)"),
                                       bank[:, 6, :]).then_inc(sums_out, 1)

                    def take_projection(b):
                        act.wait_ge(proj_ready, b + 1)
                        act.wait_ge(result_ready, b + CREDIT_RESULT)
                        nc.scalar.copy(y[:].rearrange("p t d -> p (t d)"), two_banks(2)).then_inc(proj_read, 1)

                    def root(b):
                        act.wait_ge(row_var, b + 1)
                        nc.scalar.activation(s8[:], v8[:], ACT.Sqrt).then_inc(row_std, 1)

                    def exponentials(w, wide=False, turn=True, before=True, project_of=None, root_of=None):
                        for t in range(STEPS):
                            act.wait_ge(av_done, w * STEPS + (t - 1 + CREDIT_AV))
                            for u in range(U):
                                act.wait_ge(logits_ready, w * (STEPS * U) + (t * U + u + 1))
                                nc.scalar.activation(probs[:, t % 2, u, :], logits_bank(t, u, wide),
                                                     ACT.Exp).then_inc(exp_out, 1)
                                if before and t == 0 and u == 1:
                                    take_sums(w - 1)
                                if turn and t == 1 and u == 1:
                                    take_turned(w + (LEAD - 1))
                                if project_of is not None and t == PROJECT_STEP and u == 1:
                                    take_projection(project_of)
                                if root_of is not None and t == ROOT_STEP and u == U - 1:
                                    root(root_of)

                    for v in range(LEAD - 1):
                        take_turned(v)
                    exponentials(0, before=False)
                    with act.Fori(0, 4) as i:
                        exponentials(2 * i + 1)
                        exponentials(2 * i + 2)
                    with act.Fori(0, B - 2) as b:
                        exponentials(TAIL(b), project_of=b)
                        exponentials(TAIL(b) + 1, root_of=b)
                        with act.Fori(0, 3) as i:
                            exponentials(TAIL(b) + 2 * i + 2)
                            exponentials(TAIL(b) + 2 * i + 3)
                    exponentials(TAIL(B - 2), project_of=B - 2)
                    exponentials(TAIL(B - 2) + 1, root_of=B - 2)
                    for w in range(TAIL(B - 2) + 2, NW - LEAD):
                        exponentials(w)
                    exponentials(NW - LEAD, wide=True)
                    with act.Fori(NW - LEAD + 1, NW) as w:
                        exponentials(w, wide=True, turn=False)
                    take_sums(NW - 1)
                    for h in range(2):
                        act.wait_ge(row_var, B + h)
                        nc.scalar.activation(half_of(s8, h), half_of(v8, h), ACT.Sqrt).then_inc(row_std, 1)

                @block.vector
                def _(dve):
                    v_ = nc.vector
                    v_.memset(blank[:], 0.0).then_inc(blank_ready, 1)
                    v_.memset(one_row[:], 1.0).then_inc(blank_ready, 1)
                    v_.memset(row_max[:, 0, 0:1], 0.0).then_inc(item_read, CREDIT_ITEM)
                    v_.memset(row_max[:, 0, 1:2], 0.0).then_inc(exp_out, CREDIT_EXP)
                    v_.memset(row_max[:, 0, 2:3], 0.0).then_inc(av_done, CREDIT_AV)
                    v_.memset(row_max[:, 0, 3:4], 0.0).then_inc(sums_stored, CREDIT_SUMS)
                    v_.memset(row_max[:, 0, 4:5], 0.0).then_inc(max_in, CREDIT_MAX)
                    v_.memset(row_max[:, 0, 7:8], 0.0).then_inc(unit_in, CREDIT_UNIT)
                    v_.memset(row_max[:, 0, 5:6], 0.0).then_inc(sums_out, CREDIT_PAIR)
                    v_.memset(row_max[:, 0, 6:7], 0.0).then_inc(maxT_parts, 1)
                    v_.memset(row_max[:, 0, 8:9], 0.0).then_inc(maxT_ready, CREDIT_TURNED)
                    v_.memset(row_max[:, 0, 9:10], 0.0).then_inc(result_ready, CREDIT_RESULT)

                    def reduce_item(i, v, half):
                        dve.wait_ge(item_ready, v * ITEMS + (i + 1))
                        v_.tensor_reduce(row_max[:, half, i:i + 1], two_banks(2 * (i % 2)), AX_X,
                                         ALU.max).then_inc(item_read, 1)

                    def negate(v, half):
                        dve.wait_ge(item_read, v * ITEMS + (ITEMS + CREDIT_ITEM))
                        v_.tensor_scalar(neg_max[:], row_max[:, half], -1.0, None, ALU.mult).then_inc(max_ready, 1)

                    ch = Chain(dve, tail_chain)

                    def divisors(b, part):
                        if part == 0:
                            dve.wait_ge(sums_in, b * 32 + 32)
                        cols = slice(part * P, (part + 1) * P)
                        v_.reciprocal(denom[:, cols], denom[:, cols]).then_inc(den_ready, 1)

                    def statistics(b, t):
                        if t == 0:
                            dve.wait_ge(y_ready, b + 1)
                        for i in (2 * t, 2 * t + 1):
                            ch.done(v_.bn_stats(bn2[:, i, :], y[:, i, :]))

                    def variances(b):
                        ch.settle()
                        v_.memset(spare[:], 0.0)
                        for t in range(NT):
                            ch.done(v_.bn_aggr(mean_var2[:, t, :], bn2[:, t, :]))
                        ch.settle()
                        v_.tensor_scalar(v8[:], mean_var2[:, :, 1], LN_EPS, None, ALU.add).then_inc(row_var, 1)

                    def inverse(b):
                        dve.wait_ge(row_std, b + 1)
                        ch.link(v_.reciprocal(r8[:], s8[:]))
                        ch.link(v_.tensor_tensor(r8[:], r8[:], v8[:], ALU.mult))
                        ch.link(v_.tensor_tensor(r8[:], r8[:], s8[:], ALU.add))
                        ch.link(v_.tensor_scalar(r8[:], r8[:], 0.5, None, ALU.mult))
                        v_.reciprocal(r8[:], r8[:]).then_inc(row_scale, 1)

                    def half_units(n, tail_of=None, before_tail_of=None):
                        for half in range(2):
                            v = 2 * n + 1 + half
                            for i in range(ITEMS):
                                reduce_item(i, v, 1 - half)
                                if before_tail_of is not None and half == 1 and i in (13, 15):
                                    divisors(before_tail_of, (i - 13) // 2)
                                if tail_of is None:
                                    continue
                                if half == 0 and i in (0, 2, 4, 6, 8, 10):
                                    divisors(tail_of, 2 + i // 2)
                                if half == 1 and i in (5, 7, 9, 10):
                                    statistics(tail_of, (i - 4) // 2)
                                if half == 1 and i == 11:
                                    variances(tail_of)
                                if half == 1 and i == 15:
                                    inverse(tail_of)
                            negate(v, 1 - half)

                    def first_of(b):
                        return (b + 1) * NG + 1

                    for i in range(ITEMS):
                        reduce_item(i, 0, 0)
                    negate(0, 0)
                    with dve.Fori(0, first_of(0) - 1) as n:
                        half_units(n)
                    with dve.Fori(0, B - 2) as b:
                        ch.turn(b, 2 * NT + 4)
                        half_units(first_of(b) - 1, before_tail_of=b)
                        half_units(first_of(b), tail_of=b)
                        with dve.Fori(1, NG - 1) as n:
                            half_units(first_of(b) + n)
                        ch.end_turns(B - 2)
                    half_units(first_of(B - 2) - 1, before_tail_of=B - 2)
                    half_units(first_of(B - 2), tail_of=B - 2)
                    for n in range(first_of(B - 2) + 1, NW // 2 - 1):
                        half_units(n)
                    for i in range(ITEMS):
                        reduce_item(i, NW - 1, 1)
                    negate(NW - 1, 1)

                    v = v_

                    def quotient(h):
                        dve.wait_ge(sums_in, (B + h) * 32)
                        dve.wait_ge(proj_ready, B - 1)
                        cols = slice(h * CH, (h + 1) * CH)
                        ch.link(v.reciprocal(denom[:, cols], denom[:, cols]))
                        v.tensor_tensor(outT[:, cols], numer[:, cols], denom[:, cols], ALU.mult).then_inc(outT_ready, 1)

                    def half_statistics(h):
                        dve.wait_ge(proj_ready, B + h)
                        if h == 0:
                            dve.wait_ge(result_ready, B - 1 + CREDIT_RESULT)
                        ch.link(v.tensor_tensor(half_of(y, h), bank[:, 2 + h, :].rearrange("p (t d) -> p t d", d=D),
                                                XP[:, LAST * NT + h * HT:LAST * NT + (h + 1) * HT, :], ALU.add))
                        for t in range(h * HT, (h + 1) * HT):
                            ch.done(v.bn_stats(bn2[:, t, :], y[:, t, :]))
                        ch.settle()
                        for t in range(h * HT, (h + 1) * HT):
                            ch.done(v.bn_aggr(mean_var2[:, t, :], bn2[:, t, :]))
                        ch.settle()
                        v.tensor_scalar(half_of(v8, h), half_of(mean_var2, h)[:, :, 1], LN_EPS, None,
                                        ALU.add).then_inc(row_var, 1)

                    def half_normalise(h):
                        dve.wait_ge(row_std, B + h)
                        r, yh = half_of(r8, h), half_of(y, h)
                        ch.link(v.reciprocal(r, half_of(s8, h)))
                        ch.link(v.tensor_tensor(r, r, half_of(v8, h), ALU.mult))
                        ch.link(v.tensor_tensor(r, r, half_of(s8, h), ALU.add))
                        ch.link(v.tensor_scalar(r, r, 0.5, None, ALU.mult))
                        ch.link(v.reciprocal(r, r))
                        ch.link(v.tensor_tensor(yh, yh, half_of(mean_var2, h)[:, :, 0].unsqueeze(2).to_broadcast([P, HT, D]),
                                                ALU.subtract))
                        ch.link(v.tensor_tensor(yh, yh, r.unsqueeze(2).to_broadcast([P, HT, D]), ALU.mult))
                        ch.link(v.tensor_tensor(yh, yh, gam_row[:].unsqueeze(1).to_broadcast([P, HT, D]), ALU.mult))
                        dve.wait_ge(result_out, (B - 1) * 16)
                        v.tensor_tensor(half_of(result, h), yh, X[:, LAST * NT + h * HT:LAST * NT + (h + 1) * HT, :],
                                        ALU.add).then_inc(result_ready, 1)

                    quotient(0)
                    half_statistics(0)
                    half_normalise(0)
                    quotient(1)
                    half_statistics(1)
                    half_normalise(1)

                @block.gpsimd
                def _(pool):
                    ch = Chain(pool, pool_chain)

                    def stage_v(u, t):
                        pool.wait_ge(av_done, u * (NC * STEPS) + (t + 1))
                        pool.wait_ge(ones_set, 1)
                        at = bass.ds(((u >> 2) & (B - 1)) * NT + t, 1)
                        nc.gpsimd.tensor_copy(VS[:, t, :, 0:DK],
                                              V[:, at, bass.ds((u & (NG - 1)) * (U * DK), U * DK)].rearrange(
                                                  "p o (u d) -> p (o u) d", d=DK)).then_inc(v_staged, 1)

                    def split_max(v):
                        pool.wait_ge(maxT_ready, v + 1 + CREDIT_TURNED)
                        pool.wait_ge(max_in, v * (PARTS * 16) + CREDIT_MAX)
                        pool.wait_ge(ones_set, 1)
                        ch.link(nc.gpsimd.tensor_tensor(max_parts[:, 0, :], maxT[:], zeros[:], ALU.add))
                        ch.link(nc.gpsimd.tensor_tensor(max_rest[:], maxT[:], max_parts[:, 0, :], ALU.subtract))
                        ch.link(nc.gpsimd.tensor_tensor(max_parts[:, 1, :], max_rest[:], zeros[:], ALU.add))
                        nc.gpsimd.tensor_tensor(max_parts[:, 2, :], max_rest[:], max_parts[:, 1, :],
                                                ALU.subtract).then_inc(maxT_parts, 1)

                    nc.gpsimd.memset(zeros[:], 0.0)
                    nc.gpsimd.memset(VS[:], 1.0).then_inc(ones_set, 1)
                    for t in range(STEPS):
                        stage_v(0, t)
                    split_max(0)
                    tt = nc.gpsimd.tensor_tensor

                    def add_bias(b):
                        pool.wait_ge(xp_in, 16)
                        xp = XP[:, bass.ds(b * NT, NT), :]
                        tt(xp, xp, over_rows(bo_row), ALU.add).then_inc(xpb_ready, 1)

                    def divide(b):
                        pool.wait_ge(den_ready, b * NT + NT)
                        tt(outT[:], numer[:], denom[:], ALU.mult).then_inc(outT_ready, 1)

                    def residual(b):
                        pool.wait_ge(proj_read, b + 1)
                        pool.wait_ge(xpb_ready, B)
                        tt(y[:], y[:], XP[:, bass.ds(b * NT, NT), :], ALU.add).then_inc(y_ready, 1)

                    def normalise(b):
                        pool.wait_ge(row_scale, b + 1)
                        ch.link(tt(y[:], y[:], over_channels(mean_var2[:, :, 0]), ALU.subtract))
                        ch.link(tt(y[:], y[:], over_channels(r8[:]), ALU.mult))
                        ch.link(tt(y[:], y[:], over_rows(gam_row), ALU.mult))
                        if not (isinstance(b, int) and b == 0):
                            pool.wait_ge(result_out, b * 16)
                        tt(result[:], y[:], X[:, bass.ds(b * NT, NT), :], ALU.add).then_inc(result_ready, 1)

                    def unit(u, start_of=None, end_of=None):
                        split_max(2 * u + 1)
                        if end_of is not None:
                            normalise(end_of)
                        stage_v(u + 1, 0)
                        stage_v(u + 1, 1)
                        split_max(2 * u + 2)
                        if start_of is not None:
                            divide(start_of)
                        for t in range(2, STEPS):
                            stage_v(u + 1, t)
                            if start_of is not None and t == PROJECT_STEP:
                                residual(start_of)

                    assert B == NG
                    with pool.Fori(0, NG) as u:
                        ch.turn(u, 2 * 3)
                        unit(u)
                        add_bias(u)
                        ch.end_turns(NG)

                    def batch(b, first=False, last=False):
                        unit((b + 1) * NG, start_of=b)
                        unit((b + 1) * NG + 1, end_of=b)
                        for g in range(2, NG - 1 if last else NG):
                            unit((b + 1) * NG + g)

                    batch(0)
                    with pool.Fori(1, B - 2) as b:
                        ch.turn(b - 1, NG * 6 + 3)
                        batch(b)
                        ch.end_turns(B - 3)
                    batch(B - 2, last=True)
                    split_max(NW - 1)


def kernel(**inputs):
    import numpy as np
    import concourse.bacc as bacc
    from concourse.bass_utils import run_bass_kernel_spmd as run

    def take(name):
        return np.asarray(inputs[name])

    nc = bacc.Bacc("TRN2", target_bir_lowering=False, num_devices=1)
    laid = {
        "x": take("L0_attn_x"), "rby": take("L0_attn_rby"),
        "wqT": take("L0_attn_Wq").T, "bq": take("L0_attn_bq").reshape(P, 1),
        "wkT": take("L0_attn_Wk").T, "bk": take("L0_attn_bk").reshape(P, 1),
        "wvT": take("L0_attn_Wv").T, "bv": take("L0_attn_bv"),
        "woT": take("L0_attn_Wo").T, "bo": take("L0_attn_bo"),
        "gamma": take("L0_attn_ln_gamma"), "beta": take("L0_attn_ln_beta"),
        "gate_w": take("L0_ffn_gate_w"), "gate_b": take("L0_ffn_gate_b"),
        "w1": take("L0_ffn_w1"), "b1T": take("L0_ffn_b1").reshape(E, FT, P).transpose(2, 0, 1),
        "w2": take("L0_ffn_w2"), "b2T": take("L0_ffn_b2").T,
        "ident_in": np.eye(P, dtype=np.float32),
        "freq": np.power(np.float32(10000.0), 2.0 * np.arange(0, D, 2, dtype=np.float32) / np.float32(D)).astype(np.float32),
        "pos": (np.arange(P, dtype=np.float32)[:, None] + np.float32(P) * np.arange(NT, dtype=np.float32)[None, :]),
        "rank_in": np.arange(E, 0, -1).astype(np.float32),
    }
    arrays, args = {}, []
    for name, a in laid.items():
        arrays[f"in_{name}"] = np.ascontiguousarray(a)
        args.append(nc.dram_tensor(f"in_{name}", arrays[f"in_{name}"].shape, mybir.dt.from_np(a.dtype),
                                   kind="ExternalInput").ap())
    out = nc.dram_tensor("out_0", (B, S, D), F32, kind="ExternalOutput").ap()
    build(nc, *args, out)
    return run(nc, [arrays], core_ids=[0]).results[0]["out_0"]
```
